# Optimizing a Trainium2 kernel written in Bass

```python
import numpy as np
import jax
import jax.numpy as jnp

def _softmax(x, axis=-1):
    return jax.nn.softmax(x, axis=axis)

def _gelu(x):
    return jax.nn.gelu(x, approximate=True)

def _silu(x):
    return jax.nn.silu(x)

def _sigmoid(x):
    return jax.nn.sigmoid(x)

def _layernorm(x, axis=-1, eps=1e-05):
    m = jnp.mean(x, axis=axis, keepdims=True)
    v = jnp.var(x, axis=axis, keepdims=True)
    return (x - m) / jnp.sqrt(v + eps)

def _scatter_add(tgt, idx, src, axis=0):
    return tgt.at[idx].add(src)

def _segment_sum(src, seg, n):
    return jax.ops.segment_sum(src, seg, n)
kernel_name = 'mk_flamingo_gated_d2_seqx_r8_8001a4'

def setup_inputs(seed: int=0):
    np.random.seed(seed)
    _w = jnp.asarray

    def _rec_inputs():
        import jax
        import jax.numpy as jnp
        _rk = jax.random.key(seed)
        x = -0.0005146 + 1 * jax.random.normal(jax.random.fold_in(_rk, 1), (16, 64, 128), jnp.float32)
        _lenS = 64 - jax.random.randint(jax.random.fold_in(_rk, 7), (16,), 0, max(1, 64 // 4) + 1, jnp.int32)
        _lenS2 = 64 - jax.random.randint(jax.random.fold_in(_rk, 8), (16,), 0, max(1, 64 // 4) + 1, jnp.int32)
        _ctx_768P = jax.random.normal(jax.random.fold_in(_rk, 11), (16, 16, 96), jnp.float32)
        _ctx_768c = jax.random.dirichlet(jax.random.fold_in(_rk, 511), 0.3 * jnp.ones((16,), jnp.float32), (16, 64))
        _ctx_768t = jnp.einsum('bsk,bkd->bsd', _ctx_768c, _ctx_768P)
        _ctx_768t = _ctx_768t * jax.lax.rsqrt(jnp.mean(jnp.square(_ctx_768t)) + 1e-12) * 0.953939
        ctx_768 = -0.00040386 + 0.999972 * (_ctx_768t + 0.3 * jax.random.normal(jax.random.fold_in(_rk, 611), (16, 64, 96), jnp.float32))
        _validS = jnp.arange(64)[None, :] < _lenS[:, None]
        _validS2 = jnp.arange(64)[None, :] < _lenS2[:, None]
        _causal = jnp.tril(jnp.ones((64, 64), dtype=bool))
        mask_BxS2_bk0 = jnp.logical_not(jnp.broadcast_to(_validS2[:, :], (16, 64)))
        _g = jax.random.normal(jax.random.fold_in(_rk, 9001), (2, 2), jnp.float32)
        _g = jnp.sign(_g) * jnp.maximum(jnp.abs(_g), 1.0) + (_g == 0) * 1.0
        g_xattn = _g[0]
        g_ffn = _g[1]
        return (x, ctx_768, mask_BxS2_bk0, g_xattn, g_ffn)
    x, ctx_768, mask_BxS2_bk0, g_xattn, g_ffn = _rec_inputs()

    def _L0_xattn_setup():
        import jax, jax.numpy as jnp
        import numpy as np
        DIM_IN, DIM_LAT, DIM_HEAD = (96, 128, 64)
        INNER = max(DIM_LAT, DIM_IN)
        HEADS = INNER // DIM_HEAD
        SCALE = DIM_HEAD ** (-0.5)
        RMS_EPS = 1e-08
        LN_EPS = 1e-05

        def layernorm(x, g, b):
            mu = jnp.mean(x, axis=-1, keepdims=True)
            var = jnp.mean((x - mu) ** 2, axis=-1, keepdims=True)
            return (x - mu) * jax.lax.rsqrt(var + LN_EPS) * g + b

        def rmsnorm(x, gamma):
            norm = jnp.sqrt(jnp.sum(x * x, axis=-1, keepdims=True)) * x.shape[-1] ** (-0.5)
            return x / jnp.maximum(norm, RMS_EPS) * gamma
        key = jax.random.key(seed)
        ks = jax.random.split(key, 12)
        b, n, m = (4, 512, 64)
        x = jax.random.normal(ks[0], (b, n, DIM_IN), jnp.float32)
        latents = jax.random.normal(ks[1], (b, m, DIM_LAT), jnp.float32)
        mask = jax.random.randint(ks[2], (b, n), 0, 2).astype(bool)
        s = lambda k, sh, fan: jax.random.normal(k, sh, jnp.float32) * fan ** (-0.5)
        return {'x': x, 'latents': latents, 'mask': mask, 'ln_x_g': jnp.ones((DIM_IN,), jnp.float32), 'ln_x_b': jnp.zeros((DIM_IN,), jnp.float32), 'ln_l_g': jnp.ones((DIM_LAT,), jnp.float32), 'ln_l_b': jnp.zeros((DIM_LAT,), jnp.float32), 'qn_g': jnp.ones((DIM_HEAD,), jnp.float32), 'kn_g': jnp.ones((DIM_HEAD,), jnp.float32), 'Wq': s(ks[3], (INNER, DIM_LAT), DIM_LAT), 'Wkv': s(ks[4], (2 * INNER, DIM_IN), DIM_IN), 'Wlkv': s(ks[5], (2 * INNER, DIM_LAT), DIM_LAT), 'Wo': s(ks[6], (DIM_LAT, INNER), INNER), 'bo': jnp.zeros((DIM_LAT,), jnp.float32)}
    _L0_xattn_all = _L0_xattn_setup()
    _L0_xattn_in = {k: v for k, v in _L0_xattn_all.items() if k in ('ln_x_g', 'ln_x_b', 'ln_l_g', 'ln_l_b', 'qn_g', 'kn_g', 'Wq', 'Wkv', 'Wlkv', 'Wo', 'bo')}
    del _L0_xattn_all

    def _L0_ffn_setup():
        import jax, jax.numpy as jnp
        import numpy as np
        B, S, D_MODEL, D_HIDDEN = (4, 256, 128, 512)

        def act_quant(x):
            scale = 127.0 / jnp.clip(jnp.max(jnp.abs(x), axis=-1, keepdims=True), 1e-05)
            return jnp.clip(jnp.round(x * scale), -128, 127) / scale

        def weight_quant(w):
            scale = 1.0 / jnp.clip(jnp.mean(jnp.abs(w)), 1e-05)
            return jnp.clip(jnp.round(w * scale), -1, 1) / scale

        def bit_linear(x, w):
            xq = x + jax.lax.stop_gradient(act_quant(x) - x)
            wq = w + jax.lax.stop_gradient(weight_quant(w) - w)
            return jnp.einsum('bsd,hd->bsh', xq, wq)

        def depthwise_conv1d(x_bcl, w, b):
            y = jax.lax.conv_general_dilated(x_bcl, w, window_strides=(1,), padding=[(1, 1)], dimension_numbers=('NCH', 'OIH', 'NCH'), feature_group_count=x_bcl.shape[1])
            return y + b[None, :, None]
        key = jax.random.key(seed)
        ks = jax.random.split(key, 5)
        lim1 = 1.0 / np.sqrt(D_MODEL)
        lim2 = 1.0 / np.sqrt(D_HIDDEN)
        limc = 1.0 / np.sqrt(3.0)
        return {'x': jax.random.normal(ks[0], (B, S, D_MODEL), dtype=jnp.float32), 'w1': jax.random.uniform(ks[1], (D_HIDDEN, D_MODEL), jnp.float32, -lim1, lim1), 'conv_w': jax.random.uniform(ks[2], (D_HIDDEN, 1, 3), jnp.float32, -limc, limc), 'conv_b': jax.random.uniform(ks[3], (D_HIDDEN,), jnp.float32, -limc, limc), 'w2': jax.random.uniform(ks[4], (D_MODEL, D_HIDDEN), jnp.float32, -lim2, lim2)}
    _L0_ffn_all = _L0_ffn_setup()
    _L0_ffn_in = {k: v for k, v in _L0_ffn_all.items() if k in ('w1', 'conv_w', 'conv_b', 'w2')}
    del _L0_ffn_all

    def _L1_xattn_setup():
        import jax, jax.numpy as jnp
        import numpy as np
        HEADS = 16
        DIM_HEAD = 64
        key = jax.random.key(seed)
        ks = jax.random.split(key, 7)
        b, n, m = (2, 256, 128)
        query_dim, context_dim = (128, 96)
        inner = HEADS * DIM_HEAD
        s_q = 1.0 / np.sqrt(query_dim)
        s_c = 1.0 / np.sqrt(context_dim)
        s_i = 1.0 / np.sqrt(inner)
        return {'x': jax.random.normal(ks[0], (b, n, query_dim), jnp.float32), 'context': jax.random.normal(ks[1], (b, m, context_dim), jnp.float32), 'Wq': jax.random.normal(ks[2], (query_dim, inner), jnp.float32) * s_q, 'Wk': jax.random.normal(ks[3], (context_dim, inner), jnp.float32) * s_c, 'Wv': jax.random.normal(ks[4], (context_dim, inner), jnp.float32) * s_c, 'Wo': jax.random.normal(ks[5], (inner, query_dim), jnp.float32) * s_i, 'bo': jax.random.normal(ks[6], (query_dim,), jnp.float32) * 0.01}
    _L1_xattn_all = _L1_xattn_setup()
    _L1_xattn_in = {k: v for k, v in _L1_xattn_all.items() if k in ('Wq', 'Wk', 'Wv', 'Wo', 'bo')}
    del _L1_xattn_all

    def _L1_ffn_setup():
        import jax, jax.numpy as jnp
        import numpy as np
        NUM_EXPERTS = 8
        TOP_K = 2
        ROUTE_SCALE = 1.0
        DIM = 128
        HID = 128
        B, S = (2, 512)
        key = jax.random.key(seed)
        ks = jax.random.split(key, 9)
        sc = 0.05
        return {'x': jax.random.normal(ks[0], (B, S, DIM), dtype=jnp.float32), 'gate_w': jax.random.normal(ks[1], (NUM_EXPERTS, DIM), dtype=jnp.float32) * sc, 'w1': jax.random.normal(ks[2], (NUM_EXPERTS, HID, DIM), dtype=jnp.float32) * sc, 'w2': jax.random.normal(ks[3], (NUM_EXPERTS, DIM, HID), dtype=jnp.float32) * sc, 'w3': jax.random.normal(ks[4], (NUM_EXPERTS, HID, DIM), dtype=jnp.float32) * sc, 'sw1': jax.random.normal(ks[5], (HID, DIM), dtype=jnp.float32) * sc, 'sw2': jax.random.normal(ks[6], (DIM, HID), dtype=jnp.float32) * sc, 'sw3': jax.random.normal(ks[7], (HID, DIM), dtype=jnp.float32) * sc, 'expert_bias': jnp.zeros((NUM_EXPERTS,), dtype=jnp.float32)}
    _L1_ffn_all = _L1_ffn_setup()
    _L1_ffn_in = {k: v for k, v in _L1_ffn_all.items() if k in ('gate_w', 'w1', 'w2', 'w3', 'sw1', 'sw2', 'sw3', 'expert_bias')}
    del _L1_ffn_all
    return {'x': x, 'ctx_768': ctx_768, 'mask_BxS2_bk0': mask_BxS2_bk0, 'g_xattn': g_xattn, 'g_ffn': g_ffn, 'L0_xattn_ln_x_g': _L0_xattn_in['ln_x_g'], 'L0_xattn_ln_x_b': _L0_xattn_in['ln_x_b'], 'L0_xattn_ln_l_g': _L0_xattn_in['ln_l_g'], 'L0_xattn_ln_l_b': _L0_xattn_in['ln_l_b'], 'L0_xattn_qn_g': _L0_xattn_in['qn_g'], 'L0_xattn_kn_g': _L0_xattn_in['kn_g'], 'L0_xattn_Wq': _L0_xattn_in['Wq'], 'L0_xattn_Wkv': _L0_xattn_in['Wkv'], 'L0_xattn_Wlkv': _L0_xattn_in['Wlkv'], 'L0_xattn_Wo': _L0_xattn_in['Wo'], 'L0_xattn_bo': _L0_xattn_in['bo'], 'L0_ffn_w1': _L0_ffn_in['w1'], 'L0_ffn_conv_w': _L0_ffn_in['conv_w'], 'L0_ffn_conv_b': _L0_ffn_in['conv_b'], 'L0_ffn_w2': _L0_ffn_in['w2'], 'L1_xattn_Wq': _L1_xattn_in['Wq'], 'L1_xattn_Wk': _L1_xattn_in['Wk'], 'L1_xattn_Wv': _L1_xattn_in['Wv'], 'L1_xattn_Wo': _L1_xattn_in['Wo'], 'L1_xattn_bo': _L1_xattn_in['bo'], 'L1_ffn_gate_w': _L1_ffn_in['gate_w'], 'L1_ffn_w1': _L1_ffn_in['w1'], 'L1_ffn_w2': _L1_ffn_in['w2'], 'L1_ffn_w3': _L1_ffn_in['w3'], 'L1_ffn_sw1': _L1_ffn_in['sw1'], 'L1_ffn_sw2': _L1_ffn_in['sw2'], 'L1_ffn_sw3': _L1_ffn_in['sw3'], 'L1_ffn_expert_bias': _L1_ffn_in['expert_bias']}

def reference(x, ctx_768, mask_BxS2_bk0, g_xattn, g_ffn, L0_xattn_ln_x_g, L0_xattn_ln_x_b, L0_xattn_ln_l_g, L0_xattn_ln_l_b, L0_xattn_qn_g, L0_xattn_kn_g, L0_xattn_Wq, L0_xattn_Wkv, L0_xattn_Wlkv, L0_xattn_Wo, L0_xattn_bo, L0_ffn_w1, L0_ffn_conv_w, L0_ffn_conv_b, L0_ffn_w2, L1_xattn_Wq, L1_xattn_Wk, L1_xattn_Wv, L1_xattn_Wo, L1_xattn_bo, L1_ffn_gate_w, L1_ffn_w1, L1_ffn_w2, L1_ffn_w3, L1_ffn_sw1, L1_ffn_sw2, L1_ffn_sw3, L1_ffn_expert_bias):
    import jax
    import jax.numpy as jnp

    def _L0_xattn_ref(x, latents, mask, ln_x_g, ln_x_b, ln_l_g, ln_l_b, qn_g, kn_g, Wq, Wkv, Wlkv, Wo, bo):
        import jax, jax.numpy as jnp
        import numpy as np
        DIM_IN, DIM_LAT, DIM_HEAD = (96, 128, 64)
        INNER = max(DIM_LAT, DIM_IN)
        HEADS = INNER // DIM_HEAD
        SCALE = DIM_HEAD ** (-0.5)
        RMS_EPS = 1e-08
        LN_EPS = 1e-05

        def layernorm(x, g, b):
            mu = jnp.mean(x, axis=-1, keepdims=True)
            var = jnp.mean((x - mu) ** 2, axis=-1, keepdims=True)
            return (x - mu) * jax.lax.rsqrt(var + LN_EPS) * g + b

        def rmsnorm(x, gamma):
            norm = jnp.sqrt(jnp.sum(x * x, axis=-1, keepdims=True)) * x.shape[-1] ** (-0.5)
            return x / jnp.maximum(norm, RMS_EPS) * gamma
        b, n, _ = x.shape
        m = latents.shape[1]
        xn = layernorm(x, ln_x_g, ln_x_b)
        ln = layernorm(latents, ln_l_g, ln_l_b)
        q = ln @ Wq.T
        kv = jnp.concatenate([xn @ Wkv.T, ln @ Wlkv.T], axis=1)
        k, v = (kv[..., :INNER], kv[..., INNER:])
        split_heads = lambda t: t.reshape(t.shape[0], t.shape[1], HEADS, DIM_HEAD).transpose(0, 2, 1, 3)
        q, k, v = (split_heads(q), split_heads(k), split_heads(v))
        qn = rmsnorm(q, qn_g) * SCALE
        kn = rmsnorm(k, kn_g)
        attn = jnp.einsum('bhid,bhjd->bhij', qn, kn)
        full_mask = jnp.pad(mask, ((0, 0), (0, m)), constant_values=True)
        attn = jnp.where(full_mask[:, None, None, :], attn, -jnp.finfo(attn.dtype).max)
        attn = jax.nn.softmax(attn, axis=-1)
        out = jnp.einsum('bhij,bhjd->bhid', attn, v)
        out = out.transpose(0, 2, 1, 3).reshape(b, m, INNER)
        return out @ Wo.T + bo

    def _L0_ffn_ref(x, w1, conv_w, conv_b, w2):
        import jax, jax.numpy as jnp
        import numpy as np
        B, S, D_MODEL, D_HIDDEN = (4, 256, 128, 512)

        def act_quant(x):
            scale = 127.0 / jnp.clip(jnp.max(jnp.abs(x), axis=-1, keepdims=True), 1e-05)
            return jnp.clip(jnp.round(x * scale), -128, 127) / scale

        def weight_quant(w):
            scale = 1.0 / jnp.clip(jnp.mean(jnp.abs(w)), 1e-05)
            return jnp.clip(jnp.round(w * scale), -1, 1) / scale

        def bit_linear(x, w):
            xq = x + jax.lax.stop_gradient(act_quant(x) - x)
            wq = w + jax.lax.stop_gradient(weight_quant(w) - w)
            return jnp.einsum('bsd,hd->bsh', xq, wq)

        def depthwise_conv1d(x_bcl, w, b):
            y = jax.lax.conv_general_dilated(x_bcl, w, window_strides=(1,), padding=[(1, 1)], dimension_numbers=('NCH', 'OIH', 'NCH'), feature_group_count=x_bcl.shape[1])
            return y + b[None, :, None]
        h = bit_linear(x, w1)
        h = depthwise_conv1d(h.transpose(0, 2, 1), conv_w, conv_b)
        h = h.transpose(0, 2, 1)
        h = jax.nn.silu(h)
        return bit_linear(h, w2)

    def _L1_xattn_ref(x, context, Wq, Wk, Wv, Wo, bo):
        import jax, jax.numpy as jnp
        import numpy as np
        HEADS = 16
        DIM_HEAD = 64
        b, n, _ = x.shape
        h, d = (HEADS, DIM_HEAD)
        scale = d ** (-0.5)
        q = (x @ Wq).reshape(b, n, h, d).transpose(0, 2, 1, 3)
        k = (context @ Wk).reshape(b, -1, h, d).transpose(0, 2, 1, 3)
        v = (context @ Wv).reshape(b, -1, h, d).transpose(0, 2, 1, 3)
        sim = jnp.einsum('bhid,bhjd->bhij', q, k) * scale
        attn = jax.nn.softmax(sim, axis=-1)
        out = jnp.einsum('bhij,bhjd->bhid', attn, v)
        out = out.transpose(0, 2, 1, 3).reshape(b, n, h * d)
        return out @ Wo + bo

    def _L1_ffn_ref(x, gate_w, w1, w2, w3, sw1, sw2, sw3, expert_bias):
        import jax, jax.numpy as jnp
        import numpy as np
        NUM_EXPERTS = 8
        TOP_K = 2
        ROUTE_SCALE = 1.0
        DIM = 128
        HID = 128
        B, S = (2, 512)
        bs, slen, dim = x.shape
        xf = x.reshape(-1, dim)
        scores = jax.nn.sigmoid((xf @ gate_w.T).astype(jnp.float32))
        _, sel = jax.lax.top_k(scores + expert_bias[None, :], TOP_K)
        top_scores = jnp.take_along_axis(scores, sel, axis=1) * ROUTE_SCALE
        flat_sel = sel.reshape(-1)
        order = jnp.argsort(flat_sel, stable=True)
        scores_sorted = top_scores.reshape(-1)[order]
        tok_idx = order // TOP_K
        expert_ids = flat_sel[order]
        routed = xf[tok_idx]
        routed = (routed.astype(jnp.float32) * scores_sorted[:, None]).astype(x.dtype)
        out_r = jnp.zeros_like(routed)
        for e in range(NUM_EXPERTS):
            m = (expert_ids == e)[:, None]
            h = jax.nn.silu(routed @ w1[e].T) * (routed @ w3[e].T)
            out_r = out_r + jnp.where(m, h @ w2[e].T, jnp.zeros((), routed.dtype))
        shared = jax.nn.silu(xf @ sw1.T) * (xf @ sw3.T) @ sw2.T
        out_r = (out_r.astype(jnp.float32) * scores_sorted[:, None]).astype(x.dtype)
        out = shared.at[tok_idx].add(out_r)
        return out.reshape(bs, slen, dim)
    x = x + jnp.tanh(g_xattn[0]) * _L0_xattn_ref(ctx_768, _layernorm(x, axis=-1), mask_BxS2_bk0, L0_xattn_ln_x_g, L0_xattn_ln_x_b, L0_xattn_ln_l_g, L0_xattn_ln_l_b, L0_xattn_qn_g, L0_xattn_kn_g, L0_xattn_Wq, L0_xattn_Wkv, L0_xattn_Wlkv, L0_xattn_Wo, L0_xattn_bo)
    x = x + jnp.tanh(g_ffn[0]) * _L0_ffn_ref(_layernorm(x, axis=-1), L0_ffn_w1, L0_ffn_conv_w, L0_ffn_conv_b, L0_ffn_w2)
    x = x + jnp.tanh(g_xattn[1]) * _L1_xattn_ref(_layernorm(x, axis=-1), ctx_768, L1_xattn_Wq, L1_xattn_Wk, L1_xattn_Wv, L1_xattn_Wo, L1_xattn_bo)
    x = x + jnp.tanh(g_ffn[1]) * _L1_ffn_ref(_layernorm(x, axis=-1), L1_ffn_gate_w, L1_ffn_w1, L1_ffn_w2, L1_ffn_w3, L1_ffn_sw1, L1_ffn_sw2, L1_ffn_sw3, L1_ffn_expert_bias)
    return x

_drawn_inputs = setup_inputs


def setup_inputs(seed=0):
    import zlib

    import numpy as np

    out = dict(_drawn_inputs(seed))
    spreads = {'g_ffn': (-1.0, 0.6),
     'L0_xattn_ln_x_g': (1.0, 0.6),
     'L0_xattn_ln_x_b': (0.0, 0.737),
     'L0_xattn_ln_l_g': (1.0, 0.2),
     'L0_xattn_ln_l_b': (0.0, 0.1),
     'L0_xattn_qn_g': (1.0, 0.6),
     'L0_xattn_kn_g': (1.0, 0.6),
     'L0_xattn_bo': (0.0, 0.1),
     'L1_ffn_expert_bias': (0.0, 1.369)}
    factors = {'L1_xattn_bo': 6.353, 'L1_ffn_gate_w': 2.699}
    for name, (base, spread) in spreads.items():
        noise = np.random.default_rng([zlib.crc32(name.encode()), seed]).standard_normal(out[name].shape)
        drawn = base * np.exp(spread * noise) if base else spread * noise
        out[name] = jnp.asarray(drawn.astype(out[name].dtype))
    for name, factor in factors.items():
        out[name] = (out[name] * factor).astype(out[name].dtype)
    return out
```

```python
B, S, D, DC = 16, 64, 128, 96
P = 128
T = B * S // P
HALF = T // 2
HD = 64
H1 = 16
E = 8
EN = E + 1
HID0 = 512
C0 = HID0 // P
C1 = H1 * HD // P
LN_EPS = 1e-5
MAGIC = 1.5 * 2.0**23
BIG = -3.0e38
VA = HD + 1


def halves_first(*names):
    return [(n, g) for g in range(2) for n in names]


def pe_order():
    o = []
    o += halves_first("cnT", "lnT")
    o += [("wsum", 0)]
    o += [("kT1", 0, c) for c in range(4)]
    for t in range(T):
        o += [("qkv0", t), ("ckv0", t)]
        if t % 2 == 0:
            o += [("v1", t // 2, 0), ("v1", t // 2, 1)]
        if t >= 2:
            o += [("qkT0", t - 2)]
    o += [("qkT0", T - 2), ("qkT0", T - 1)]
    for r in range(T // 2):
        o += [("sm0", r, 0), ("sm0", r, 1), ("kT1", 0, 4 + r)]
        if r >= 1:
            o += [("sT0", r - 1, 0), ("sT0", r - 1, 1)]
    o += [("sT0", T // 2 - 1, 0), ("sT0", T // 2 - 1, 1)]
    o += [("pv0", t) for t in range(T)]
    o += [("oT0", 0), ("oT0", 1), ("y0", 0), ("y0", 1)]
    o += [("kT1", 1, c) for c in range(4)]
    o += [("v1", t, j) for t in range(HALF, T) for j in range(2)]
    o += [("xqT", 0), ("xqT", 1)]
    o += [("h0", g, c) for g in range(2) for c in range(C0)]
    o += [("kT1", 1, c) for c in range(4, 8)]
    o += [("amT", 0), ("amT", 1), ("s2b", 0), ("s2b", 1), ("f0", 0), ("f0", 1)]
    o += [("xT1", 0), ("xT1", 1)]
    o += [("qT1", g, c) for g in range(2) for c in range(C1)]
    for i in range(2 * T + 8):
        if i < 2 * T:
            o += [("sm1", i)]
        if 0 <= i - 2 < 2 * T:
            o += [("sT1", i - 2)]
        if 0 <= i - 4 < 2 * T:
            o += [("pv1", i - 4, 0), ("pv1", i - 4, 1)]
        j = i - 6
        if 0 <= j < 2 * T and j % 2 == 1:
            o += [("oT1", j // 2, 0), ("oT1", j // 2, 1)]
        j = i - 8
        if 0 <= j < 2 * T and j % 2 == 1:
            o += [("y1", j // 2)]
    o = o + [("y1", T - 1)] if ("y1", T - 1) not in o else o
    o += [("xT3", 0), ("xT3", 1), ("gate", 0), ("gate", 1)]
    for i in range(3 * T + 3):
        if i < 3 * T:
            o += [("G", i), ("U", i)]
        if 0 <= i - 2 < 3 * T:
            o += [("hT", i - 2)]
        if i >= 5 and (i - 3) % 3 == 2:
            o += [("f1", (i - 3) // 3)]
    return o


PE_ORDER = pe_order()
BANKS = 8
SLOT = {key: (n % BANKS, n // BANKS + 1) for n, key in enumerate(PE_ORDER)}
assert len(SLOT) == len(PE_ORDER)


def build_program(nc, x_d, ctx_d, ctxT_d, mask_d, w0_d, wc_d, wq1_d, wo1_d, w1_d, w3_d, w2_d, gate_d,
                  cols_d, cols96_d, rows_d, out_d):
    from contextlib import ExitStack

    from concourse import mybir

    f32, bf16, u8 = mybir.dt.float32, mybir.dt.bfloat16, mybir.dt.uint8
    ALU, ACT, AX = mybir.AluOpType, mybir.ActivationFunctionType, mybir.AxisListType

    stack = ExitStack()
    with stack:
        def sb(name, shape, dt=f32):
            return stack.enter_context(nc.sbuf_tensor(name, shape, dt))

        sems = {}

        def sem(name):
            sems[name] = stack.enter_context(nc.semaphore(name))
            return sems[name]

        x = sb("x", [P, T, D])
        ctx = sb("ctx", [P, T, DC])
        ctxT = sb("ctxT", [DC, T * P])
        w0 = sb("w0", [P, 384 + 128 + 512 + 512])
        w_qlkv, w_o0 = w0[:, 0:384], w0[:, 384:512]
        w_up, w_down = w0[:, 512:1024], w0[:, 1024:1536]
        wc_all = sb("wc", [P, 256 + 1024 + 1024])
        wc = wc_all[0:DC, :]
        w_ckv, w_k1, w_v1 = wc[:, 0:256], wc[:, 256:1280], wc[:, 1280:2304]
        w_q1 = sb("w_q1", [P, 1024])
        w_o1 = sb("w_o1", [P, C1, D])
        w1, w3 = wc_all[:, 0:EN * 128], wc_all[:, EN * 128:2 * EN * 128]
        w2 = w0[:, 0:EN * D].rearrange("p (e d) -> p e d", d=D)
        w_gate = sb("w_gate", [P, E])
        cols = sb("cols", [P, 4 + 12 + 4])
        lnl_g, lnl_b, qn_g, kn_g = (cols[:, i:i + 1] for i in range(4))
        conv_w = cols[:, 4:16].rearrange("p (c k) -> p c k", k=3)
        conv_b = cols[:, 16:20]
        cols96 = sb("cols96", [DC, 2])
        rows = sb("rows", [P, 128 + 128 + E + 4])
        bo0, bo1, e_bias, gates_raw = rows[:, 0:128], rows[:, 128:256], rows[:, 256:264], rows[:, 264:268]

        ident = sb("ident", [P, P])
        ident64 = sb("ident64", [P, HD], bf16)
        blockones = sb("blockones", [P, P], bf16)
        onesf = sb("onesf", [P, P])
        ones_row = sb("ones_row", [1, P], bf16)
        minus_half = sb("minus_half", [P, 8])
        before = sb("before", [P, E, E])

        gates = sb("gates", [P, 4])
        gq = sb("gq", [P, 1])
        stats = sb("stats", [P, T, 6])
        cstats = sb("cstats", [P, T, 6])
        mv = sb("mv", [P, 4, T, 2])
        cmv = sb("cmv", [P, T, 2])
        ln_s = sb("ln_s", [P, 4, T])
        ln_b = sb("ln_b", [P, 4, T])
        ln_w = sb("ln_w", [P, 4, T])
        ln_u = sb("ln_u", [P, T])
        c_s = sb("c_s", [P, T])
        c_b = sb("c_b", [P, T])
        wabs = sb("wabs", [P, 2])
        wsc = sb("wsc", [P, 2])
        winv = sb("winv", [P, 2])
        conv_ws = sb("conv_ws", [P, C0, 3])
        w_upq = sb("w_upq", [P, 512])
        w_downq = sb("w_downq", [P, C0, D], bf16)

        region = sb("region", [P, 14368])

        def part(at, *shape, dt=f32):
            size = 1
            for n in shape:
                size *= n
            words = size // (2 if dt is bf16 else 1)
            v = region[:, at:at + words]
            v = v.bitcast(bf16) if dt is bf16 else v
            names = "abcd"[:len(shape)]
            if len(shape) == 1:
                return v
            return v.rearrange(f"p ({' '.join(names)}) -> p {' '.join(names)}",
                               **dict(zip(names[1:], shape[1:])))

        w_tmp = part(12320, 1024)
        mask8 = w_upq[0:1, 0:256].bitcast(u8)
        mask_row = region[0:1, 13344:14368].bitcast(bf16).rearrange("p (g b k) -> p g b k", b=B, g=2)

        xn = sb("xn", [P, T, D])
        xl = xn
        cn = sb("cn", [P, T, DC])
        lnT = sb("lnT", [P, T * P])
        xT1 = sb("xT1", [P, T * P])
        cnT = xT1[0:DC, :]
        sq = part(4096, T, 6, HD)
        ss = sb("ss", [P, T, 6])
        rq = sb("rq", [P, T, 6])
        qkn = sq
        v0 = part(10240, T * 2, 2, VA)
        qT0 = part(7168, T, P)
        kT0 = part(8192, T, 2, P)
        nm0 = sb("nm0", [P, T, 2], bf16)
        D0 = sb("D0", [P, T, 2, HD], bf16)
        PT0 = part(0, T, 2, 2, P)
        rs0 = sb("rs0", [P, T, 2])
        o0 = part(12320, T, D)
        oT0 = part(13344, T * P)
        xb = sb("xb", [P, T, D])
        x1 = sb("x1", [P, T, D])

        am = sb("am", [P, T])
        s1 = sb("s1", [P, T])
        i1 = sb("i1", [P, T])
        xq = part(12320, T, D)
        xqT = lnT
        qT1 = sb("qT1", [P, C1, T * P])
        y, z = qT1[:, 0:C0, :], qT1[:, C0:C1, :]
        amh = xb[:, :, :].rearrange("p t d -> p (t d)")
        am2 = sb("am2", [P, T])
        s2 = sb("s2", [P, T])
        i2 = sb("i2", [P, T])
        zs = y
        zq = part(11328, C0, T * P, dt=bf16)
        x2 = x

        kT1 = sb("kT1", [P, C1, T * P])
        v1_halves = (sb("v1a", [P, HALF, H1, VA]), part(0, HALF, H1, VA))
        nm1 = sb("nm1", [P, 2 * T, C1], bf16)
        ctx_flat = ctx[:, :, :].rearrange("p t d -> p (t d)")
        D1 = ctx_flat[:, 0:512].bitcast(bf16).rearrange("p (i c q) -> p i c q", i=2, c=C1)
        PT1 = part(4160, 3, C1, P)
        rs1 = sb("rs1", [P, 2 * T, C1])
        o1 = part(7232, 2 * C1, 2, HD)
        oT1 = part(9280, 2, C1, P)
        x3 = x1

        xT3 = xT1
        ez = sb("ez", [P, T, E])
        sc = sb("sc", [P, T, E])
        biased = sb("biased", [P, T, E])
        gt = ctx_flat[:, 512:576].rearrange("p (e f) -> p e f", f=E)
        eq = ctx_flat[:, 576:640].rearrange("p (e f) -> p e f", f=E)
        rank = sb("rank", [P, T, E])
        cw = sb("cw", [P, T, E])
        cw2 = sb("cw2", [P, T, E])
        sl = part(0, 3, 512)
        h = part(1536, 3, 512)
        hT = part(3072, 4, 4, P)
        outb = part(5120, T, D)

        bank = [stack.enter_context(nc.psum_tensor(f"bank{i}", [P, 512], f32)) for i in range(BANKS)]
        filled = [sem(f"filled{i}") for i in range(BANKS)]
        taken_sem = [sem(f"taken{i}") for i in range(BANKS)]

        def ps(key):
            return bank[SLOT[key][0]]

        def full(eng, key):
            eng.wait_ge(filled[SLOT[key][0]], SLOT[key][1])

        def take(ins, key):
            ins.then_inc(taken_sem[SLOT[key][0]], 1)

        def taken(eng, key):
            eng.wait_ge(taken_sem[SLOT[key][0]], SLOT[key][1])

        for name in """in_x in_ctx in_ctxT in_mask in_w0 in_wc in_wq1 in_wo1 in_w1 in_w3 in_w2 in_gate
                in_cols in_cols96 in_rows out_done consts dve_step pool_step act_step stats_done rstd_done
                xl_done cn_done lnT_done cnT_done gates_done mask_done gq_done wabs_done w_up_done
                w_down_done conv_done sq_done v0_done ss_done rq_done qkn_done qT0_done kT0_done nm0_done
                D0_done PT0_done o0_done oT0_done xb_done x1_done xq_done xqT_done y_done conv_y_done z_done
                amh_done s2_done zq_done x2_done xn1_done xT1_done qT1_done kT1_done v1_done nm1_done
                D1_done PT1_done o1_done oT1_done x3_done xn3_done xT3_done ez_done cw_done sl_done
                h_done hT_done f1_done pv1_read""".split():
            sem(name)
        s = sems
        block = stack.enter_context(nc.Block())

        @block.sync
        def _(sp):
            sp.dma_start(x[:, :, :], x_d.rearrange("(t p) d -> p t d", p=P)).then_inc(s["in_x"], 16)
            sp.dma_start(w0[:, :], w0_d).then_inc(s["in_w0"], 16)
            sp.dma_start(w_q1[:, :], wq1_d).then_inc(s["in_wq1"], 16)
            sp.dma_start(w_o1[:, :, :], wo1_d.rearrange("(c p) d -> p c d", p=P)).then_inc(s["in_wo1"], 16)
            sp.dma_start(w_gate[:, :], gate_d).then_inc(s["in_gate"], 16)
            full(sp, ("kT1", 1, C1 - 1))
            sp.dma_start(w1[:, :], w1_d).then_inc(s["in_w1"], 16)
            sp.dma_start(w3[:, :], w3_d).then_inc(s["in_w3"], 16)
            full(sp, ("y0", 1))
            sp.wait_ge(s["w_down_done"], 1)
            sp.dma_start(w2[:, :, :], w2_d.rearrange("p (e d) -> p e d", d=D)).then_inc(s["in_w2"], 16)
            out_v = out_d.rearrange("(t p) d -> p t d", p=P)
            for t in range(T):
                taken(sp, ("f1", t))
                sp.dma_start(out_v[:, t, :], outb[:, t, :]).then_inc(s["out_done"], 16)
            sp.wait_ge(s["out_done"], 16 * T)

        @block.gpsimd
        def _(pool):
            steps = [0]

            def link(ins):
                steps[0] += 1
                ins.then_inc(s["pool_step"], 1)
                pool.wait_ge(s["pool_step"], steps[0])

            announced = dict(consts=0, rstd_done=0, rq_done=0, D0_done=0, xb_done=0, D1_done=0)

            def announce(ins, name):
                announced[name] += 1
                ins.then_inc(s[name], 1)
                pool.wait_ge(s[name], announced[name])

            link(pool.memset(ident[:, :], 0.0))
            link(pool.affine_select(out=ident[:, :], in_=ident[:, :], compare_op=ALU.not_equal, fill=1.0,
                                    base=0, pattern=[[-1, P]], channel_multiplier=1))
            link(pool.memset(minus_half[:, :], -0.5))
            announce(pool.memset(onesf[:, :], 1.0), "consts")

            def rstd(var, out_ap, n):
                link(pool.tensor_scalar(out_ap, var, LN_EPS, None, ALU.add))
                link(pool.tensor_tensor(out_ap, out_ap, minus_half[:, 0:n], ALU.pow))

            def finish_ln(k, g):
                tt = slice(g * HALF, (g + 1) * HALF)
                mean, var = mv[:, k, tt, 0], mv[:, k, tt, 1]
                pool.wait_ge(s["stats_done"], 2 * k + g + 1)
                rstd(var, ln_s[:, k, tt], HALF)
                if k == 0:
                    u = ln_u[:, tt]
                    link(pool.tensor_tensor(u, ln_s[:, 0, tt], ln_s[:, 0, tt], ALU.mult))
                    link(pool.tensor_tensor(u, u, var, ALU.mult))
                    rstd(u, u, HALF)
                    link(pool.tensor_tensor(ln_s[:, 0, tt], ln_s[:, 0, tt], u, ALU.mult))
                    rstd(cmv[:, tt, 1], c_s[:, tt], HALF)
                    link(pool.tensor_tensor(c_b[:, tt], cmv[:, tt, 0], c_s[:, tt], ALU.mult))
                    link(pool.tensor_scalar(c_b[:, tt], c_b[:, tt], -1.0, None, ALU.mult))
                link(pool.tensor_tensor(ln_w[:, k, tt], mean, ln_s[:, k, tt], ALU.mult))
                announce(pool.tensor_scalar(ln_b[:, k, tt], ln_w[:, k, tt], -1.0, None, ALU.mult), "rstd_done")

            finish_ln(0, 0)
            finish_ln(0, 1)
            link(pool.memset(ident64[:, :], 0.0))
            link(pool.affine_select(out=ident64[:, :], in_=ident64[:, :], compare_op=ALU.not_equal, fill=1.0,
                                    base=0, pattern=[[-1, HD]], channel_multiplier=1))
            link(pool.affine_select(out=ident64[:, :], in_=ident64[:, :], compare_op=ALU.not_equal, fill=1.0,
                                    base=-HD, pattern=[[-1, HD]], channel_multiplier=1))
            link(pool.memset(blockones[:, :], 0.0))
            for b in range(2):
                link(pool.memset(blockones[b * HD:(b + 1) * HD, b * HD:(b + 1) * HD], 1.0))
            link(pool.memset(ones_row[:, :], 1.0))
            link(pool.memset(before[:, :, :], 1.0))
            link(pool.affine_select(out=before[:, :, :], in_=before[:, :, :], compare_op=ALU.is_gt, fill=0.0,
                                    base=0, pattern=[[1, E], [-1, E]], channel_multiplier=0))
            for b in range(2):
                other = slice((1 - b) * HD, (2 - b) * HD)
                rows_b = slice(b * HD, (b + 1) * HD)
                link(pool.memset(PT0[rows_b, :, :, :, other], 0.0))
            link(pool.memset(v0[:, :, :, HD:VA], 1.0))
            announce(pool.memset(v1_halves[0][:, :, :, HD:VA], 1.0), "consts")

            for t in range(T):
                pool.wait_ge(s["ss_done"], t + 1)
                link(pool.tensor_scalar(rq[:, t, :], ss[:, t, :], 1.0 / HD, 1e-16, ALU.mult, ALU.max))
                announce(pool.tensor_tensor(rq[:, t, :], rq[:, t, :], minus_half[:, 0:6], ALU.pow), "rq_done")
            for r in range(T // 2):
                taken(pool, ("sm0", r, 0))
                taken(pool, ("sm0", r, 1))
                for t in (2 * r, 2 * r + 1):
                    announce(pool.tensor_tensor(
                        D0[:, t, :, :], ident64[:, :].unsqueeze(1).broadcast_to([P, 2, HD]),
                        nm0[:, t, :].unsqueeze(2).broadcast_to([P, 2, HD]), ALU.mult), "D0_done")
            pool.wait_ge(s["gates_done"], 1)
            pool.wait_ge(s["in_rows"], 16)
            for k, bo in ((0, bo0), (1, bo1)):
                link(pool.tensor_scalar(bo, bo, gates[:, k:k + 1], None, ALU.mult))
            for g in range(2):
                tt = slice(g * HALF, (g + 1) * HALF)
                announce(pool.tensor_tensor(xb[:, tt, :], x[:, tt, :], bo0.unsqueeze(1).broadcast_to([P, HALF, D]),
                                   ALU.add), "xb_done")
            taken(pool, ("oT0", 1))
            for b in range(2):
                other = slice((1 - b) * HD, (2 - b) * HD)
                rows_b = slice(b * HD, (b + 1) * HD)
                link(pool.memset(PT1[rows_b, :, :, other], 0.0))
            announce(pool.memset(v1_halves[1][:, :, :, HD:VA], 1.0), "consts")
            for g in range(2):
                finish_ln(1, g)
            for g in range(2):
                finish_ln(2, g)
            for g in range(2):
                tt = slice(g * HALF, (g + 1) * HALF)
                announce(pool.tensor_tensor(xb[:, tt, :], x2[:, tt, :], bo1.unsqueeze(1).broadcast_to([P, HALF, D]),
                                   ALU.add), "xb_done")
            for i in range(2 * T):
                taken(pool, ("sm1", i))
                if i >= 2:
                    full(pool, ("sT1", i - 2))
                announce(pool.tensor_tensor(
                    D1[:, i % 2, :, :], ident64[:, :].unsqueeze(1).broadcast_to([P, C1, HD]),
                    nm1[:, i, :].unsqueeze(2).broadcast_to([P, C1, HD]), ALU.mult), "D1_done")
            for g in range(2):
                finish_ln(3, g)

        @block.scalar
        def _(act):
            act.dma_start(ctx[:, :, :], ctx_d.rearrange("(t p) d -> p t d", p=P)).then_inc(s["in_ctx"], 16)
            act.dma_start(cols[:, :], cols_d).then_inc(s["in_cols"], 16)
            act.dma_start(cols96[:, :], cols96_d).then_inc(s["in_cols96"], 16)
            act.dma_start(rows[:, :], rows_d.broadcast_to([P, 268])).then_inc(s["in_rows"], 16)
            act.dma_start(mask8[:, :], mask_d).then_inc(s["in_mask"], 16)
            act.dma_start(wc[:, :], wc_d).then_inc(s["in_wc"], 16)
            act.dma_start(ctxT[:, :], ctxT_d).then_inc(s["in_ctxT"], 16)

            act.wait_ge(s["in_rows"], 16)
            act.activation(gates[:, :], gates_raw, ACT.Tanh).then_inc(s["gates_done"], 1)
            act.wait_ge(s["in_cols96"], 16)
            act.wait_ge(s["in_cols"], 16)
            for g in range(2):
                tok = slice(g * 512, (g + 1) * 512)
                full(act, ("cnT", g))
                i = act.activation(cnT[:, tok], ps(("cnT", g))[0:DC, :], ACT.Identity, scale=cols96[:, 0:1],
                                   bias=cols96[:, 1:2])
                take(i, ("cnT", g))
                full(act, ("lnT", g))
                i = act.activation(lnT[:, tok], ps(("lnT", g))[:, :], ACT.Identity, scale=lnl_g, bias=lnl_b)
                take(i, ("lnT", g))

            def take_kT1(g, c):
                full(act, ("kT1", g, c))
                take(act.activation(kT1[:, c, g * 512:(g + 1) * 512], ps(("kT1", g, c))[:, :], ACT.Copy),
                      ("kT1", g, c))

            def take_v1(t, j):
                full(act, ("v1", t, j))
                take(act.activation(v1_halves[t // HALF][:, t % HALF, 8 * j:8 * j + 8, 0:HD],
                                     ps(("v1", t, j))[:, :].rearrange("p (h d) -> p h d", d=HD), ACT.Copy),
                      ("v1", t, j))

            act.wait_ge(s["consts"], 2)
            for c in range(4):
                take_kT1(0, c)

            def take_qkT0(t):
                key = ("qkT0", t)
                full(act, key)
                act.activation(kT0[:, t, :, :], ps(key)[:, 128:384].rearrange("p (g n) -> p g n", g=2),
                               ACT.Copy).then_inc(s["kT0_done"], 1)
                act.wait_ge(s["gq_done"], 1)
                take(act.activation(qT0[:, t, :], ps(key)[:, 0:128], ACT.Copy, scale=gq[:, 0:1]), key)

            for t in range(T):
                kq, kc = ("qkv0", t), ("ckv0", t)
                full(act, kq)
                act.activation(sq[:, t, 0:4, :], ps(kq)[:, 0:256].rearrange("p (h d) -> p h d", d=HD),
                               ACT.Square).then_inc(s["sq_done"], 1)
                act.activation(v0[:, 2 * t + 1, :, 0:HD], ps(kq)[:, 256:384].rearrange("p (h d) -> p h d", d=HD),
                               ACT.Copy).then_inc(s["v0_done"], 1)
                full(act, kc)
                act.activation(sq[:, t, 4:6, :], ps(kc)[:, 0:128].rearrange("p (h d) -> p h d", d=HD),
                               ACT.Square).then_inc(s["sq_done"], 1)
                act.activation(v0[:, 2 * t, :, 0:HD], ps(kc)[:, 128:256].rearrange("p (h d) -> p h d", d=HD),
                               ACT.Copy).then_inc(s["v0_done"], 1)
                if t % 2 == 0:
                    take_v1(t // 2, 0)
                    take_v1(t // 2, 1)
                if t >= 2:
                    take_qkT0(t - 2)
            take_qkT0(T - 2)
            take_qkT0(T - 1)

            def exp0(r, hh):
                key = ("sT0", r, hh)
                full(act, key)
                for b in range(2):
                    rb = slice(b * HD, (b + 1) * HD)
                    i = act.activation(
                        PT0[rb, 2 * r:2 * r + 2, :, hh, b * HD:(b + 1) * HD],
                        ps(key)[rb, 0:256].rearrange("p (t g q) -> p t g q", t=2, g=2), ACT.Exp)
                take(i, key)

            for r in range(T // 2):
                take_kT1(0, 4 + r)
                if r >= 1:
                    exp0(r - 1, 0)
                    exp0(r - 1, 1)
            exp0(T // 2 - 1, 0)
            exp0(T // 2 - 1, 1)
            for g in range(2):
                tok = slice(g * 512, (g + 1) * 512)
                full(act, ("oT0", g))
                take(act.activation(oT0[:, tok], ps(("oT0", g))[:, :], ACT.Copy), ("oT0", g))
            for c in range(4):
                take_kT1(1, c)
            for t in range(HALF, T):
                take_v1(t, 0)
                take_v1(t, 1)
            for g in range(2):
                tok = slice(g * 512, (g + 1) * 512)
                full(act, ("xqT", g))
                take(act.activation(xqT[:, tok], ps(("xqT", g))[:, :], ACT.Copy), ("xqT", g))

            def silu0(g, c):
                taken(act, ("h0", g, c))
                act.activation(z[:, c, g * 512:(g + 1) * 512], y[:, c, g * 512:(g + 1) * 512],
                               ACT.Silu).then_inc(s["z_done"], 1)

            act.wait_ge(s["conv_done"], 1)
            pairs = [(g, c) for g in range(2) for c in range(C0)]
            for n, (g, c) in enumerate(pairs):
                full(act, ("h0", g, c))
                act.activation(y[:, c, g * 512:(g + 1) * 512], ps(("h0", g, c))[:, :], ACT.Identity,
                               scale=conv_ws[:, c, 1:2], bias=conv_b[:, c:c + 1]).then_inc(s["y_done"], 1)
                if n >= 1:
                    silu0(*pairs[n - 1])
            silu0(*pairs[-1])
            for c in range(4, 8):
                take_kT1(1, c)
            for g in range(2):
                tok = slice(g * 512, (g + 1) * 512)
                full(act, ("xT1", g))
                take(act.activation(xT1[:, tok], ps(("xT1", g))[:, :], ACT.Copy), ("xT1", g))
            for g in range(2):
                for c in range(0, C1, 2):
                    full(act, ("qT1", g, c))
                    take(act.activation(qT1[:, c, g * 512:(g + 1) * 512], ps(("qT1", g, c))[:, :], ACT.Copy,
                                         scale=HD**-0.5), ("qT1", g, c))

            def take_oT1(t):
                if t >= 2:
                    full(act, ("y1", t - 2))
                for j in range(2):
                    full(act, ("oT1", t, j))
                    take(act.activation(oT1[:, t % 2, 4 * j:4 * j + 4, :],
                                         ps(("oT1", t, j))[:, :].rearrange("p (c n) -> p c n", n=P), ACT.Copy),
                          ("oT1", t, j))

            for i in range(2 * T + 6):
                n = i - 2
                if 0 <= n < 2 * T:
                    key = ("sT1", n)
                    full(act, key)
                    if n >= 3:
                        full(act, ("pv1", n - 3, 1))
                    for b in range(2):
                        rb = slice(b * HD, (b + 1) * HD)
                        last = act.activation(PT1[rb, n % 3, :, b * HD:(b + 1) * HD],
                                           ps(key)[rb, :].rearrange("p (c q) -> p c q", q=HD), ACT.Exp)
                    take(last, key)
                j = i - 6
                if 0 <= j < 2 * T and j % 2 == 1:
                    take_oT1(j // 2)
            for g in range(2):
                tok = slice(g * 512, (g + 1) * 512)
                full(act, ("xT3", g))
                take(act.activation(xT3[:, tok], ps(("xT3", g))[:, :], ACT.Copy), ("xT3", g))
            for g in range(2):
                full(act, ("gate", g))
                take(act.activation(ez[:, g * HALF:(g + 1) * HALF, :],
                                     ps(("gate", g))[:, 0:32].rearrange("p (t e) -> p t e", e=E), ACT.Exp,
                                     scale=-1.0), ("gate", g))

            def take_hT(i):
                if i >= 4:
                    full(act, ("f1", (i - 4) // 3))
                n = 1 if i % 3 == 2 else 4
                full(act, ("hT", i))
                take(act.activation(hT[:, i % 4, 0:n, :],
                                     ps(("hT", i))[:, 0:n * P].rearrange("p (e n) -> p e n", n=P), ACT.Copy),
                      ("hT", i))

            act.wait_ge(s["cw_done"], 2)
            for i in range(3 * T):
                t, j = divmod(i, 3)
                key = ("G", i)
                full(act, key)
                if i >= 3:
                    taken(act, ("U", i - 3))
                for e in range(4 if j < 2 else 1):
                    k = slice(e * 128, (e + 1) * 128)
                    if j < 2:
                        n = act.activation(sl[:, i % 3, k], ps(key)[:, k], ACT.Silu,
                                           scale=cw[:, t, 4 * j + e:4 * j + e + 1])
                    else:
                        n = act.activation(sl[:, i % 3, k], ps(key)[:, k], ACT.Silu)
                take(n, key)
                if i >= 2:
                    take_hT(i - 2)
            take_hT(3 * T - 2)
            take_hT(3 * T - 1)

        @block.vector
        def _(dve):
            steps = [0]

            def link(ins):
                steps[0] += 1
                ins.then_inc(s["dve_step"], 1)
                dve.wait_ge(s["dve_step"], steps[0])

            def ln_stats(k, g, src):
                tiles = range(g * HALF, (g + 1) * HALF)
                for t in tiles:
                    i = dve.bn_stats(stats[:, t, :], src[:, t, :])
                link(i)
                for t in tiles:
                    i = dve.bn_aggr(mv[:, k, t, :], stats[:, t, :])
                i.then_inc(s["stats_done"], 1)

            dve.wait_ge(s["in_x"], 16)
            dve.wait_ge(s["in_ctx"], 16)
            for g in range(2):
                tiles = range(g * HALF, (g + 1) * HALF)
                for t in tiles:
                    i = dve.bn_stats(cstats[:, t, :], ctx[:, t, :])
                link(i)
                for t in tiles:
                    i = dve.bn_aggr(cmv[:, t, :], cstats[:, t, :])
                ln_stats(0, g, x)
            for g in range(2):
                dve.wait_ge(s["rstd_done"], g + 1)
                for t in range(g * HALF, (g + 1) * HALF):
                    i = dve.tensor_scalar(cn[:, t, :], ctx[:, t, :], c_s[:, t:t + 1], c_b[:, t:t + 1],
                                          ALU.mult, ALU.add)
                i.then_inc(s["cn_done"], 1)
                for t in range(g * HALF, (g + 1) * HALF):
                    i = dve.tensor_scalar(xl[:, t, :], x[:, t, :], ln_s[:, 0, t:t + 1], ln_b[:, 0, t:t + 1],
                                          ALU.mult, ALU.add)
                i.then_inc(s["xl_done"], 1)

            dve.wait_ge(s["in_mask"], 16)
            link(dve.memset(mask_row[:, :, :, :], 0.0))
            dve.tensor_scalar(mask_row[:, 0, :, :], mask8[:, :].rearrange("p (b k) -> p b k", k=S), 1.0, -BIG,
                              ALU.subtract, ALU.mult)\
               .then_inc(s["mask_done"], 1)
            dve.wait_ge(s["in_cols"], 16)
            dve.scalar_tensor_tensor(gq[:, :], qn_g, HD**-0.5, kn_g, ALU.mult, ALU.mult).then_inc(s["gq_done"], 1)

            dve.wait_ge(s["in_w0"], 16)
            dve.tensor_reduce(wabs[:, 0:1], w_up, AX.X, ALU.add, apply_absolute_value=True)
            dve.tensor_reduce(wabs[:, 1:2], w_down, AX.X, ALU.add, apply_absolute_value=True)\
               .then_inc(s["wabs_done"], 1)
            full(dve, ("wsum", 0))
            i = dve.tensor_scalar(winv[:, :], ps(("wsum", 0))[:, 0:2], 1.0 / (D * HID0), 1e-5, ALU.mult, ALU.max)
            take(i, ("wsum", 0))
            taken(dve, ("wsum", 0))
            link(dve.reciprocal(wsc[:, :], winv[:, :]))
            for k, wsrc in enumerate((w_up, w_down)):
                tmp = w_tmp[:, 512 * k:512 * k + 512]
                link(dve.tensor_scalar(tmp, wsrc, wsc[:, k:k + 1], MAGIC, ALU.mult, ALU.add))
                link(dve.tensor_scalar(tmp, tmp, MAGIC, 1.0, ALU.subtract, ALU.min))
            dve.tensor_scalar(w_upq[:, :], w_tmp[:, 0:512], -1.0, None, ALU.max).then_inc(s["w_up_done"], 1)
            dve.tensor_scalar(w_downq[:, :, :], w_tmp[:, 512:1024].rearrange("p (c d) -> p c d", d=D), -1.0,
                              None, ALU.max).then_inc(s["w_down_done"], 1)
            dve.tensor_scalar(conv_ws[:, :, :], conv_w, winv[:, 0:1], None, ALU.mult).then_inc(s["conv_done"], 1)

            def norm_qk(t):
                kq, kc = ("qkv0", t), ("ckv0", t)
                dve.wait_ge(s["rq_done"], t + 1)
                dve.wait_ge(s["v0_done"], 2 * t + 2)
                take(dve.tensor_tensor(qkn[:, t, 0:4, :], ps(kq)[:, 0:256].rearrange("p (h d) -> p h d", d=HD),
                                        rq[:, t, 0:4].unsqueeze(2).broadcast_to([P, 4, HD]), ALU.mult), kq)
                take(dve.tensor_tensor(qkn[:, t, 4:6, :], ps(kc)[:, 0:128].rearrange("p (h d) -> p h d", d=HD),
                                        rq[:, t, 4:6].unsqueeze(2).broadcast_to([P, 2, HD]), ALU.mult), kc)

            for t in range(T):
                dve.wait_ge(s["sq_done"], 2 * t + 2)
                dve.tensor_reduce(ss[:, t, :], sq[:, t, :, :], AX.X, ALU.add).then_inc(s["ss_done"], 1)
                if t >= 1:
                    norm_qk(t - 1)
            norm_qk(T - 1)

            for r in range(T // 2):
                for hh in range(2):
                    key = ("sm0", r, hh)
                    full(dve, key)
                    take(dve.tensor_reduce(nm0[:, 2 * r:2 * r + 2, hh],
                                          ps(key)[:, 0:256].rearrange("p (t k) -> p t k", t=2), AX.X, ALU.max,
                                          negate=True), key)

            for t in range(T):
                key = ("pv0", t)
                full(dve, key)
                o_ps = ps(key)[:, 0:2 * VA].rearrange("p (h d) -> p h d", d=VA)
                link(dve.reciprocal(rs0[:, t, :], o_ps[:, :, HD]))
                take(dve.tensor_tensor(o0[:, t, :].rearrange("p (h d) -> p h d", d=HD), o_ps[:, :, 0:HD],
                                        rs0[:, t, :].unsqueeze(2).broadcast_to([P, 2, HD]), ALU.mult), key)
            dve.wait_ge(s["gates_done"], 1)
            for g in range(2):
                key = ("y0", g)
                tt = slice(g * HALF, (g + 1) * HALF)
                full(dve, key)
                dve.wait_ge(s["xb_done"], g + 1)
                i = dve.scalar_tensor_tensor(x1[:, tt, :], ps(key)[:, :].rearrange("p (t d) -> p t d", d=D),
                                             gates[:, 0:1], xb[:, tt, :], ALU.mult, ALU.add)
                take(i, key)
                taken(dve, key)
                ln_stats(1, g, x1)

            def apply_ln(k, t, src, dst):
                return dve.tensor_scalar(dst[:, t, :], src[:, t, :], ln_s[:, k, t:t + 1], ln_b[:, k, t:t + 1],
                                         ALU.mult, ALU.add)

            for g in range(2):
                tiles = range(g * HALF, (g + 1) * HALF)
                tt = slice(g * HALF, (g + 1) * HALF)
                dve.wait_ge(s["rstd_done"], 3 + g)
                for t in tiles:
                    i = apply_ln(1, t, x1, xn)
                link(i)
                link(dve.tensor_reduce(am[:, tt], xn[:, tt, :], AX.X, ALU.max, apply_absolute_value=True))
                link(dve.tensor_scalar(i1[:, tt], am[:, tt], 1e-5, 1.0 / 127.0, ALU.max, ALU.mult))
                link(dve.reciprocal(s1[:, tt], i1[:, tt]))
                for t in tiles:
                    i = dve.tensor_scalar(xn[:, t, :], xn[:, t, :], s1[:, t:t + 1], MAGIC, ALU.mult, ALU.add)
                link(i)
                for t in tiles:
                    i = dve.tensor_scalar(xq[:, t, :], xn[:, t, :], MAGIC, i1[:, t:t + 1], ALU.subtract, ALU.mult)
                i.then_inc(s["xq_done"], 1)
            for g in range(2):
                for c in range(C0):
                    key = ("h0", g, c)
                    hv = ps(key)[:, :].rearrange("p (b n) -> p b n", n=S)
                    yv = y[:, c, g * 512:(g + 1) * 512].rearrange("p (b n) -> p b n", n=S)
                    dve.wait_ge(s["y_done"], g * C0 + c + 1)
                    link(dve.scalar_tensor_tensor(yv[:, :, 1:S], hv[:, :, 0:S - 1], conv_ws[:, c, 0:1],
                                                  yv[:, :, 1:S], ALU.mult, ALU.add))
                    i = dve.scalar_tensor_tensor(yv[:, :, 0:S - 1], hv[:, :, 1:S], conv_ws[:, c, 2:3],
                                                 yv[:, :, 0:S - 1], ALU.mult, ALU.add)
                    take(i, key)
            for g in range(2):
                tok = slice(g * 512, (g + 1) * 512)
                dve.wait_ge(s["z_done"], C0 * (g + 1))
                dve.tensor_reduce(amh[:, tok], z[:, :, tok].rearrange("p c n -> p n c"), AX.X, ALU.max,
                                  apply_absolute_value=True).then_inc(s["amh_done"], 1)
            for g in range(2):
                tt = slice(g * HALF, (g + 1) * HALF)
                key = ("amT", g)
                full(dve, key)
                i = dve.tensor_reduce(am2[:, tt], ps(key)[:, :].rearrange("p (t n) -> p t n", n=P), AX.X, ALU.max)
                take(i, key)
                taken(dve, key)
                link(dve.tensor_scalar(i2[:, tt], am2[:, tt], 1e-5, 1.0 / 127.0, ALU.max, ALU.mult))
                dve.reciprocal(s2[:, tt], i2[:, tt]).then_inc(s["s2_done"], 1)
                link(dve.tensor_scalar(i2[:, tt], i2[:, tt], winv[:, 1:2], gates[:, 2:3], ALU.mult, ALU.mult))
            for g in range(2):
                tok = slice(g * 512, (g + 1) * 512)
                key = ("s2b", g)
                full(dve, key)
                for c in range(C0):
                    i = dve.tensor_tensor(zs[:, c, tok], z[:, c, tok], ps(key)[:, :], ALU.mult)
                take(i, key)
                taken(dve, key)
                dve.tensor_scalar(zq[:, :, tok], zs[:, :, tok], MAGIC, MAGIC, ALU.add, ALU.subtract)\
                   .then_inc(s["zq_done"], 1)
            for g in range(2):
                key = ("f0", g)
                full(dve, key)
                for t in range(g * HALF, (g + 1) * HALF):
                    i = dve.scalar_tensor_tensor(x2[:, t, :], ps(key)[:, (t % HALF) * D:(t % HALF + 1) * D],
                                                 i2[:, t:t + 1], x1[:, t, :], ALU.mult, ALU.add)
                take(i, key)
                taken(dve, key)
                ln_stats(2, g, x2)
            for g in range(2):
                dve.wait_ge(s["rstd_done"], 5 + g)
                for t in range(g * HALF, (g + 1) * HALF):
                    i = apply_ln(2, t, x2, xn)
                i.then_inc(s["xn1_done"], 1)
            for g in range(2):
                for c in range(1, C1, 2):
                    full(dve, ("qT1", g, c))
                    take(dve.tensor_scalar(qT1[:, c, g * 512:(g + 1) * 512], ps(("qT1", g, c))[:, :],
                                            HD**-0.5, None, ALU.mult), ("qT1", g, c))

            def head_out(i, q):
                t, par = divmod(i, 2)
                key = ("pv1", i, q)
                full(dve, key)
                if par == 0 and q == 0 and t >= 2:
                    full(dve, ("oT1", t - 2, 1))
                o_ps = ps(key)[:, 0:4 * VA].rearrange("p (h d) -> p h d", d=VA)
                r = rs1[:, i, 4 * q:4 * q + 4]
                link(dve.reciprocal(r, o_ps[:, :, HD]))
                take(dve.tensor_tensor(o1[:, C1 * (t % 2) + 4 * q:C1 * (t % 2) + 4 * q + 4, par, :], o_ps[:, :, 0:HD],
                                        r.unsqueeze(2).broadcast_to([P, 4, HD]), ALU.mult), key)

            def add_y1(t):
                key = ("y1", t)
                full(dve, key)
                dve.wait_ge(s["xb_done"], 4)
                i = dve.scalar_tensor_tensor(x3[:, t, :], ps(key)[:, 0:D], gates[:, 1:2], xb[:, t, :],
                                             ALU.mult, ALU.add)
                take(i, key)

            for i in range(2 * T + 8):
                if i < 2 * T:
                    key = ("sm1", i)
                    full(dve, key)
                    take(dve.tensor_reduce(nm1[:, i, :], ps(key)[:, :].rearrange("p (c k) -> p c k", k=HD),
                                           AX.X, ALU.max, negate=True), key)
                j = i - 4
                if 0 <= j < 2 * T:
                    head_out(j, 0)
                    head_out(j, 1)
                j = i - 8
                if 0 <= j < 2 * T and j % 2 == 1:
                    add_y1(j // 2)
            for g in range(2):
                key = ("y1", g * HALF + HALF - 1)
                taken(dve, key)
                ln_stats(3, g, x3)
            for g in range(2):
                dve.wait_ge(s["rstd_done"], 7 + g)
                for t in range(g * HALF, (g + 1) * HALF):
                    i = apply_ln(3, t, x3, xn)
                i.then_inc(s["xn3_done"], 1)
            for g in range(2):
                tt = slice(g * HALF, (g + 1) * HALF)
                key_ = ("gate", g)
                taken(dve, key_)
                link(dve.tensor_scalar(ez[:, tt, :], ez[:, tt, :], 1.0, None, ALU.add))
                link(dve.reciprocal(sc[:, tt, :], ez[:, tt, :]))
                link(dve.tensor_tensor(biased[:, tt, :], sc[:, tt, :],
                                       e_bias.unsqueeze(1).broadcast_to([P, HALF, E]), ALU.add))
                for t in range(g * HALF, (g + 1) * HALF):
                    this = biased[:, t, :].unsqueeze(2).broadcast_to([P, E, E])
                    other = biased[:, t, :].unsqueeze(1).broadcast_to([P, E, E])
                    dve.tensor_tensor(gt[:, :, :], other, this, ALU.is_gt)
                    link(dve.tensor_tensor(eq[:, :, :], other, this, ALU.is_equal))
                    link(dve.tensor_tensor(eq[:, :, :], eq[:, :, :], before[:, :, :], ALU.mult))
                    link(dve.tensor_tensor(gt[:, :, :], gt[:, :, :], eq[:, :, :], ALU.add))
                    link(dve.tensor_reduce(rank[:, t, :], gt[:, :, :], AX.X, ALU.add))
                link(dve.scalar_tensor_tensor(cw[:, tt, :], rank[:, tt, :], 2.0, sc[:, tt, :], ALU.is_lt, ALU.mult))
                dve.tensor_tensor(cw2[:, tt, :], cw[:, tt, :], cw[:, tt, :], ALU.mult).then_inc(s["cw_done"], 1)

            def finish_tile(t):
                key = ("f1", t)
                full(dve, key)
                i = dve.scalar_tensor_tensor(outb[:, t, :], ps(key)[:, 0:D], gates[:, 3:4], x3[:, t, :],
                                             ALU.mult, ALU.add)
                take(i, key)

            dve.wait_ge(s["cw_done"], 2)
            for i in range(3 * T):
                t, j = divmod(i, 3)
                key_ = ("U", i)
                full(dve, key_)
                taken(dve, ("G", i))
                if i >= 3:
                    full(dve, ("hT", i - 3))
                for e in range(4 if j < 2 else 1):
                    k = slice(e * 128, (e + 1) * 128)
                    if j < 2:
                        n = dve.scalar_tensor_tensor(h[:, i % 3, k], ps(key_)[:, k],
                                                     cw2[:, t, 4 * j + e:4 * j + e + 1], sl[:, i % 3, k],
                                                     ALU.mult, ALU.mult)
                    else:
                        n = dve.tensor_tensor(h[:, i % 3, k], ps(key_)[:, k], sl[:, i % 3, k], ALU.mult)
                take(n, key_)
                if i >= 5 and (i - 3) % 3 == 2:
                    finish_tile((i - 3) // 3)
            finish_tile(T - 1)

        @block.tensor
        def _(pe):
            def transposes(key, src, tiles, n_out=P):
                for n, t in enumerate(tiles):
                    i = pe.transpose(ps(key)[0:n_out, n * P:(n + 1) * P], src(t), ident[:, :])
                return i

            def half(g):
                return range(g * HALF, (g + 1) * HALF), slice(g * 512, (g + 1) * 512)

            def mm(out, lhsT, rhs, start=True, stop=True):
                return pe.matmul(out, lhsT, rhs, start=start, stop=stop, skip_group_check=True)

            def batch(b):
                return slice(b * HD, (b + 1) * HD)

            def tok(t, b=None):
                return slice(t * P, (t + 1) * P) if b is None else slice(t * P + b * S, t * P + (b + 1) * S)

            pe.wait_ge(s["consts"], 1)
            for n, key in enumerate(PE_ORDER):
                name, a = key[0], key[1:]
                out = ps(key)
                if n >= BANKS:
                    taken(pe, PE_ORDER[n - BANKS])
                if name == "cnT":
                    pe.wait_ge(s["cn_done"], a[0] + 1)
                    i = transposes(key, lambda t: cn[:, t, :], half(a[0])[0], DC)
                elif name == "lnT":
                    pe.wait_ge(s["xl_done"], a[0] + 1)
                    i = transposes(key, lambda t: xl[:, t, :], half(a[0])[0])
                elif name == "wsum":
                    pe.wait_ge(s["wabs_done"], 1)
                    i = mm(out[:, 0:2], onesf[:, :], wabs[:, :])
                elif name == "kT1":
                    g, c = a
                    pe.wait_ge(s["in_wc"], 16)
                    pe.wait_ge(s["in_ctxT"], 16)
                    i = mm(out[:, :], w_k1[:, c * P:(c + 1) * P], ctxT[:, half(g)[1]])
                elif name == "v1":
                    t, j = a
                    i = mm(out[:, :], ctxT[:, tok(t)], w_v1[:, 512 * j:512 * (j + 1)])
                elif name == "qkv0":
                    t = a[0]
                    pe.wait_ge(s["in_w0"], 16)
                    taken(pe, ("lnT", t // HALF))
                    i = mm(out[:, 0:384], lnT[:, tok(t)], w_qlkv)
                elif name == "ckv0":
                    t = a[0]
                    taken(pe, ("cnT", t // HALF))
                    i = mm(out[:, 0:256], cnT[:, tok(t)], w_ckv)
                elif name == "qkT0":
                    t = a[0]
                    taken(pe, ("ckv0", t))
                    taken(pe, ("qkv0", t))
                    for m, c in enumerate((0, 2, 1)):
                        i = pe.transpose(out[:, m * P:(m + 1) * P],
                                         qkn[:, t, 2 * c:2 * c + 2, :].rearrange("p h d -> p (h d)"), ident[:, :])
                elif name == "sm0":
                    r, h_ = a
                    hr = batch(h_)
                    pe.wait_ge(s["mask_done"], 1)
                    pe.wait_ge(s["consts"], 2)
                    for b in range(2):
                        for m in range(2):
                            t = 2 * r + m
                            cols_ = slice(m * P, (m + 1) * P)
                            if m == 0:
                                taken(pe, ("qkT0", 2 * r))
                                taken(pe, ("qkT0", 2 * r + 1))
                            mm(out[batch(b), cols_], ones_row[0:1, 0:HD],
                               mask_row[0:1, :, 2 * t + b, :], start=m == 0, stop=False)
                        for m in range(2):
                            t = 2 * r + m
                            cols_ = slice(m * P, (m + 1) * P)
                            i = mm(out[batch(b), cols_], qT0[hr, t, batch(b)], kT0[hr, t, :, batch(b)], start=False)
                elif name == "sT0":
                    r, h_ = a
                    hr = batch(h_)
                    pe.wait_ge(s["D0_done"], 2 * r + 2)
                    mm(out[:, 0:256], blockones[:, :],
                       D0[:, 2 * r:2 * r + 2, h_, :].unsqueeze(2).broadcast_to([P, 2, 2, HD]), stop=False)
                    for m in range(2):
                        t = 2 * r + m
                        mm(out[:, m * P:m * P + HD], mask_row[0:1, 0, 2 * t:2 * t + 2, :].rearrange("p b k -> p (b k)"),
                           ones_row[0:1, 0:HD], start=False, stop=False)
                        for grp in range(2):
                            for b in range(2):
                                c = m * P + grp * HD
                                i = mm(out[batch(b), c:c + HD], kT0[hr, t, grp, batch(b)], qT0[hr, t, batch(b)],
                                       start=False)
                elif name == "pv0":
                    t = a[0]
                    taken(pe, ("sT0", t // 2, 0))
                    taken(pe, ("sT0", t // 2, 1))
                    for h_ in range(2):
                        for grp in range(2):
                            i = mm(out[:, h_ * VA:(h_ + 1) * VA], PT0[:, t, grp, h_, :], v0[:, 2 * t + grp, h_, :],
                                   start=grp == 0, stop=grp == 1)
                elif name == "oT0":
                    for t in half(a[0])[0]:
                        taken(pe, ("pv0", t))
                    i = transposes(key, lambda t: o0[:, t, :], half(a[0])[0])
                elif name == "y0":
                    taken(pe, ("oT0", a[0]))
                    for m, t in enumerate(half(a[0])[0]):
                        i = mm(out[:, m * D:(m + 1) * D], oT0[:, tok(t)], w_o0)
                elif name == "xqT":
                    pe.wait_ge(s["xq_done"], a[0] + 1)
                    i = transposes(key, lambda t: xq[:, t, :], half(a[0])[0])
                elif name == "h0":
                    g, c = a
                    pe.wait_ge(s["w_up_done"], 1)
                    taken(pe, ("xqT", g))
                    i = mm(out[:, :], w_upq[:, c * P:(c + 1) * P], xqT[:, half(g)[1]])
                elif name == "amT":
                    pe.wait_ge(s["amh_done"], a[0] + 1)
                    i = transposes(key, lambda t: amh[:, tok(t)], half(a[0])[0])
                elif name == "s2b":
                    pe.wait_ge(s["s2_done"], a[0] + 1)
                    for m, t in enumerate(half(a[0])[0]):
                        i = mm(out[:, m * P:(m + 1) * P], s2[:, t:t + 1].broadcast_to([P, P]), ident[:, :])
                elif name == "f0":
                    pe.wait_ge(s["zq_done"], a[0] + 1)
                    pe.wait_ge(s["w_down_done"], 1)
                    for m, t in enumerate(half(a[0])[0]):
                        for c in range(C0):
                            i = mm(out[:, m * D:(m + 1) * D], zq[:, c, tok(t)], w_downq[:, c, :], start=c == 0,
                                   stop=c == C0 - 1)
                elif name == "xT1":
                    pe.wait_ge(s["xn1_done"], a[0] + 1)
                    i = transposes(key, lambda t: xn[:, t, :], half(a[0])[0])
                elif name == "qT1":
                    g, c = a
                    pe.wait_ge(s["in_wq1"], 16)
                    taken(pe, ("xT1", g))
                    i = mm(out[:, :], w_q1[:, c * P:(c + 1) * P], xT1[:, half(g)[1]])
                elif name == "sm1":
                    t, par = divmod(a[0], 2)
                    hr = batch(par)
                    for c in range(C1):
                        taken(pe, ("qT1", t // HALF, c))
                        taken(pe, ("kT1", t // HALF, c))
                        for b in range(2):
                            i = mm(out[batch(b), c * HD:(c + 1) * HD], qT1[hr, c, tok(t, b)], kT1[hr, c, tok(t, b)])
                elif name == "sT1":
                    t, par = divmod(a[0], 2)
                    hr = batch(par)
                    pe.wait_ge(s["D1_done"], a[0] + 1)
                    mm(out[:, :], blockones[:, :], D1[:, a[0] % 2, :, :].rearrange("p c q -> p (c q)"), stop=False)
                    for c in range(C1):
                        for b in range(2):
                            i = mm(out[batch(b), c * HD:(c + 1) * HD], kT1[hr, c, tok(t, b)], qT1[hr, c, tok(t, b)],
                                   start=False)
                elif name == "pv1":
                    i1, q = a
                    t, par = divmod(i1, 2)
                    taken(pe, ("sT1", i1))
                    taken(pe, ("v1", t, 0))
                    taken(pe, ("v1", t, 1))
                    pe.wait_ge(s["consts"], 3)
                    for m in range(4):
                        c = 4 * q + m
                        i = mm(out[:, m * VA:(m + 1) * VA], PT1[:, i1 % 3, c, :], v1_halves[t // HALF][:, t % HALF, 2 * c + par, :])
                elif name == "oT1":
                    t, j = a
                    for par in range(2):
                        for q in range(2):
                            taken(pe, ("pv1", 2 * t + par, q))
                    i = transposes(key, lambda c: o1[:, C1 * (t % 2) + c, :, :].rearrange("p r d -> p (r d)"),
                                   range(4 * j, 4 * j + 4))
                elif name == "y1":
                    t = a[0]
                    pe.wait_ge(s["in_wo1"], 16)
                    taken(pe, ("oT1", t, 0))
                    taken(pe, ("oT1", t, 1))
                    for c in range(C1):
                        i = mm(out[:, 0:D], oT1[:, t % 2, c, :], w_o1[:, c, :], start=c == 0, stop=c == C1 - 1)
                elif name == "xT3":
                    pe.wait_ge(s["xn3_done"], a[0] + 1)
                    i = transposes(key, lambda t: xn[:, t, :], half(a[0])[0])
                elif name == "gate":
                    pe.wait_ge(s["in_gate"], 16)
                    taken(pe, ("xT3", a[0]))
                    for m, t in enumerate(half(a[0])[0]):
                        i = mm(out[:, m * E:(m + 1) * E], xT3[:, tok(t)], w_gate[:, :])
                elif name in ("G", "U"):
                    t, j = divmod(a[0], 3)
                    w, loaded = (w1, "in_w1") if name == "G" else (w3, "in_w3")
                    pe.wait_ge(s[loaded], 16)
                    n_out = 512 if j < 2 else 128
                    i = mm(out[:, 0:n_out], xT3[:, tok(t)], w[:, 512 * j:512 * j + n_out])
                elif name == "hT":
                    taken(pe, ("U", a[0]))
                    i = transposes(key, lambda e: h[:, a[0] % 3, e * P:(e + 1) * P],
                                   range(1 if a[0] % 3 == 2 else 4))
                elif name == "f1":
                    t = a[0]
                    pe.wait_ge(s["in_w2"], 16)
                    for e in range(EN):
                        k = 3 * t + e // 4
                        if e % 4 == 0:
                            taken(pe, ("hT", k))
                        i = mm(out[:, 0:D], hT[:, k % 4, e % 4, :], w2[:, e, :], start=e == 0, stop=e == EN - 1)
                i.then_inc(filled[SLOT[key][0]], 1)


def kernel(**inputs):
    import numpy as np
    import concourse.bacc as bacc
    from concourse import mybir
    from concourse.bass_utils import run_bass_kernel_spmd

    v = {k: np.asarray(a) for k, a in inputs.items()}
    tr = lambda a: np.ascontiguousarray(a.T)
    cat = lambda *a: np.ascontiguousarray(np.concatenate(a, axis=1))
    col = lambda a: np.asarray(a).reshape(-1, 1)
    w2_0 = tr(v["L0_ffn_w2"]).reshape(C0, P, D).transpose(1, 0, 2).reshape(P, C0 * D)
    experts = lambda w, sw: cat(*[tr(w[e]) for e in range(E)], tr(sw))
    qn, kn = v["L0_xattn_qn_g"], v["L0_xattn_kn_g"]
    arrays = {
        "x": v["x"].reshape(B * S, D),
        "ctx": v["ctx_768"].reshape(B * S, DC),
        "ctxT": tr(v["ctx_768"].reshape(B * S, DC)),
        "mask": v["mask_BxS2_bk0"].reshape(1, B * S),
        "w0": cat(tr(v["L0_xattn_Wq"]), tr(v["L0_xattn_Wlkv"]), tr(v["L0_xattn_Wo"]), tr(v["L0_ffn_w1"]), w2_0),
        "wc": cat(tr(v["L0_xattn_Wkv"]), v["L1_xattn_Wk"], v["L1_xattn_Wv"]),
        "wq1": np.ascontiguousarray(v["L1_xattn_Wq"]),
        "wo1": np.ascontiguousarray(v["L1_xattn_Wo"]),
        "w1": experts(v["L1_ffn_w1"], v["L1_ffn_sw1"]),
        "w3": experts(v["L1_ffn_w3"], v["L1_ffn_sw3"]),
        "w2": experts(v["L1_ffn_w2"], v["L1_ffn_sw2"]),
        "gate": tr(v["L1_ffn_gate_w"]),
        "cols": cat(col(v["L0_xattn_ln_l_g"]), col(v["L0_xattn_ln_l_b"]), col(np.concatenate([qn, qn])),
                    col(np.concatenate([kn, kn])),
                    v["L0_ffn_conv_w"].reshape(C0, P, 3).transpose(1, 0, 2).reshape(P, C0 * 3),
                    v["L0_ffn_conv_b"].reshape(C0, P).T),
        "cols96": cat(col(v["L0_xattn_ln_x_g"]), col(v["L0_xattn_ln_x_b"])),
        "rows": np.concatenate([v["L0_xattn_bo"], v["L1_xattn_bo"], v["L1_ffn_expert_bias"], v["g_xattn"],
                                v["g_ffn"]]).reshape(1, -1),
    }
    nc = bacc.Bacc("TRN2", target_bir_lowering=False, num_devices=1)
    args = [nc.dram_tensor(f"in_{k}_dram", a.shape, mybir.dt.from_np(a.dtype), kind="ExternalInput").ap()
            for k, a in arrays.items()]
    out = nc.dram_tensor("out_dram", (B * S, D), mybir.dt.float32, kind="ExternalOutput").ap()
    build_program(nc, *args, out)
    r = run_bass_kernel_spmd(nc, [{f"in_{k}_dram": a for k, a in arrays.items()}], core_ids=[0])
    return r.results[0]["out_dram"].reshape(B, S, D)
```

```python
B, S, D, DC = 16, 64, 128, 96
P = 128
T = B * S // P
HALF = T // 2
HD = 64
H1 = 16
E = 8
EN = E + 1
HID0 = 512
C0 = HID0 // P
C1 = H1 * HD // P
LN_EPS = 1e-5
MAGIC = 1.5 * 2.0**23
BIG = -3.0e38
VA = HD + 1


RESULT_NAMES = """cnT lnT wsum kT1 v1 qkv0 ckv0 qkT0 sm0 sT0 pv0 oT0 y0 xqT h0 amT s2b f0 xT1 qT1 sm1 sT1 pv1 oT1
    y1 xT3 gate G U hT f1""".split()

SCHEDULE = """
    constants stats.0.0 stats.0.1 rstd.0.0 rstd.0.1 norm0.0 norm0.1 biases wabs cnT.0 lnT.0 cnT.1 lnT.1 qkv0.0
    ckv0.0 qkv0.1 ckv0.1 qkv0.2 ckv0.2 norm_qk.0 qkv0.3 norm_qk.1 ckv0.3 qkv0.4 ckv0.4 wsum.0 norm_qk.2 qkv0.5
    norm_qk.3 ckv0.5 qkT0.0 qkv0.6 norm_qk.4 ckv0.6 norm_qk.5 qkv0.7 ckv0.7 norm_qk.6 xb.0.0 qkT0.1 sm0.0.0
    kT1.0.0 qkT0.2 norm_qk.7 qkT0.3 sm0.0.1 qkT0.4 qkT0.5 sm0.1.0 qkT0.6 qkT0.7 D0.0 sm0.1.1 D0.1 sm0.2.0
    sm0.2.1 sm0.3.0 sT0.0.0 sT0.0.1 sT0.1.0 D0.2 sT0.1.1 sm0.3.1 sT0.2.0 D0.3 xb.0.1 pv0.0 sT0.2.1 pv0.1 sT0.3.0
    pv0.2 pv0.3 pv0.4 oT0.0 y0.0 stats.1.0 sT0.3.1 pv0.5 rstd.1.0 pv0.6 pv0.7 oT0.1 quant.0 y0.1 xqT.0 h0.0.0
    silu0.0.0 h0.0.1 h0.0.2 h0.0.3 kT1.0.1 silu0.0.1 kT1.0.2 silu0.0.2 kT1.0.3 silu0.0.3 v1.0.0 kT1.0.4 kT1.0.5
    kT1.0.6 amh.0 kT1.0.7 v1.0.1 amT.0 zeros_PT1 s2b.0 v1.1.0 ones_v1 stats.1.1 kT1.1.0 kT1.1.1 v1.1.1 f0.0
    kT1.1.2 stats.2.0 v1.2.0 v1.2.1 rstd.2.0 rstd.1.1 norm1.0 v1.3.0 v1.3.1 kT1.1.3 xT1.0 kT1.1.4 qT1.0.0
    kT1.1.5 quant.1 qT1.0.1 qT1.0.2 qT1.0.3 qT1.0.4 qT1.0.5 qT1.0.6 qT1.0.7 v1.4.0 sm1.0 xqT.1 v1.4.1 h0.1.0
    sT1.0 silu0.1.0 xb.1.0 h0.1.1 sm1.1 sm1.2 silu0.1.1 kT1.1.6 h0.1.2 h0.1.3 pv1.0.0 pv1.0.1 silu0.1.2 sT1.1
    sT1.2 silu0.1.3 v1.5.0 v1.5.1 pv1.1.0 kT1.1.7 sm1.3 sm1.4 amh.1 v1.6.0 sT1.3 v1.6.1 amT.1 v1.7.0 pv1.1.1
    s2b.1 pv1.2.0 sm1.5 sT1.4 sm1.6 f0.1 stats.2.1 oT1.0.0 pv1.2.1 pv1.3.0 pv1.3.1 oT1.0.1 rstd.2.1 norm1.1
    xb.1.1 pv1.4.0 sT1.5 sm1.7 xT1.1 pv1.4.1 sT1.6 v1.7.1 qT1.1.0 qT1.1.1 qT1.1.2 qT1.1.3 oT1.1.0 pv1.5.0
    qT1.1.4 pv1.5.1 sT1.7 qT1.1.5 y1.0 oT1.1.1 qT1.1.6 y1.1 pv1.6.0 qT1.1.7 sm1.8 sm1.9 pv1.6.1 sT1.8 pv1.7.0
    oT1.2.0 oT1.2.1 sm1.10 sT1.9 pv1.7.1 sm1.11 pv1.8.0 pv1.8.1 sT1.10 sT1.11 pv1.9.0 pv1.9.1 oT1.3.0 oT1.3.1
    sm1.12 y1.2 pv1.10.0 sT1.12 sm1.13 oT1.4.0 y1.3 stats.3.0 oT1.4.1 rstd.3.0 pv1.10.1 pv1.11.0 pv1.11.1 sT1.13
    norm3.0 pv1.12.0 sm1.14 pv1.12.1 pv1.13.0 xT3.0 pv1.13.1 sm1.15 gate.0 router.0 sT1.14 oT1.5.0 oT1.5.1
    sT1.15 y1.4 pv1.14.0 pv1.14.1 oT1.6.0 pv1.15.0 y1.5 pv1.15.1 oT1.6.1 oT1.7.0 oT1.7.1 y1.6 y1.7 stats.3.1 G.0
    rstd.3.1 U.0 G.1 U.1 G.2 norm3.1 hT.0 U.2 G.3 U.3 hT.1 G.4 hT.2 U.4 xT3.1 G.5 U.5 gate.1 hT.3 router.1 f1.0
    hT.4 G.6 U.6 hT.5 f1.1 G.7 U.7 hT.6 G.8 G.9 U.8 U.9 hT.7 G.10 hT.8 U.10 G.11 hT.9 U.11 f1.2 hT.10 hT.11 f1.3
    G.12 U.12 G.13 G.14 U.13 U.14 hT.12 G.15 U.15 hT.13 hT.14 G.16 U.16 f1.4 hT.15 G.17 U.17 hT.16 G.18 U.18
    hT.17 G.19 U.19 f1.5 G.20 hT.18 G.21 hT.19 U.20 U.21 G.22 hT.20 U.22 G.23 U.23 hT.21 f1.6 hT.22 hT.23 f1.7
"""
ORDER = [(word.split(".")[0], *(int(n) for n in word.split(".")[1:])) for word in SCHEDULE.split()]
RESULTS = [step for step in ORDER if step[0] in RESULT_NAMES]
BANKS = 8
SLOT = {key: (n % BANKS, n // BANKS + 1) for n, key in enumerate(RESULTS)}
assert len(SLOT) == len(RESULTS)


def build_program(nc, x_d, ctx_d, ctxT_d, mask_d, w0_d, wc_d, wq1_d, wo1_d, w1_d, w3_d, w2_d, gate_d,
                  cols_d, cols96_d, rows_d, out_d):
    from contextlib import ExitStack

    from concourse import mybir

    f32, bf16, u8 = mybir.dt.float32, mybir.dt.bfloat16, mybir.dt.uint8
    ALU, ACT, AX = mybir.AluOpType, mybir.ActivationFunctionType, mybir.AxisListType

    stack = ExitStack()
    with stack:
        def sb(name, shape, dt=f32):
            return stack.enter_context(nc.sbuf_tensor(name, shape, dt))

        sems = {}

        def sem(name):
            sems[name] = stack.enter_context(nc.semaphore(name))
            return sems[name]

        x = sb("x", [P, T, D])
        ctx = sb("ctx", [P, T, DC])
        ctxT = sb("ctxT", [DC, T * P])
        w0 = sb("w0", [P, 384 + 128 + 512 + 512])
        w_qlkv, w_o0 = w0[:, 0:384], w0[:, 384:512]
        w_up, w_down = w0[:, 512:1024], w0[:, 1024:1536]
        wc_all = sb("wc", [P, 256 + 1024 + 1024])
        wc = wc_all[0:DC, :]
        w_ckv, w_k1, w_v1 = wc[:, 0:256], wc[:, 256:1280], wc[:, 1280:2304]
        w_q1 = sb("w_q1", [P, 1024])
        w_o1 = sb("w_o1", [P, C1, D])
        w1, w3 = wc_all[:, 0:EN * 128], wc_all[:, EN * 128:2 * EN * 128]
        w2 = w0[:, 0:EN * D].rearrange("p (e d) -> p e d", d=D)
        w_gate = sb("w_gate", [P, E])
        cols = sb("cols", [P, 4 + 12 + 4])
        lnl_g, lnl_b, qn_g, kn_g = (cols[:, i:i + 1] for i in range(4))
        conv_w = cols[:, 4:16].rearrange("p (c k) -> p c k", k=3)
        conv_b = cols[:, 16:20]
        cols96 = sb("cols96", [DC, 2])
        rows = sb("rows", [P, 128 + 128 + E + 4])
        bo0, bo1, e_bias, gates_raw = rows[:, 0:128], rows[:, 128:256], rows[:, 256:264], rows[:, 264:268]

        ident = sb("ident", [P, P])
        ident64 = sb("ident64", [P, HD], bf16)
        blockones = sb("blockones", [P, P], bf16)
        onesf = sb("onesf", [P, P])
        ones_row = sb("ones_row", [1, P], bf16)
        minus_half = sb("minus_half", [P, 2, HALF])
        minus_half_row = minus_half[:, :, :].rearrange("p a b -> p (a b)")
        before = sb("before", [P, E, E])

        gates = sb("gates", [P, 4])
        gq = sb("gq", [P, 1])
        stats = sb("stats", [P, T, 6])
        cstats = sb("cstats", [P, T, 6])
        mv = sb("mv", [P, 4, T, 2])
        cmv = sb("cmv", [P, T, 2])
        ln_s = sb("ln_s", [P, 5, T])
        c_s = ln_s[:, 0, :]
        wabs = sb("wabs", [P, 2])
        wsc = sb("wsc", [P, 2])
        winv = sb("winv", [P, 2])
        conv_ws = sb("conv_ws", [P, C0, 3])
        w_upq = sb("w_upq", [P, 512])
        w_downq = sb("w_downq", [P, C0, D], bf16)

        regions = [sb(f"region{g}", [P, 7184]) for g in range(2)]

        def part(g, at, *shape, dt=f32):
            size = 1
            for n in shape:
                size *= n
            words = size // (2 if dt is bf16 else 1)
            v = regions[g][:, at:at + words]
            v = v.bitcast(bf16) if dt is bf16 else v
            names = "abcd"[:len(shape)]
            if len(shape) == 1:
                return v
            return v.rearrange(f"p ({' '.join(names)}) -> p {' '.join(names)}",
                               **dict(zip(names[1:], shape[1:])))

        mask8 = w_upq[0:1, 0:256].bitcast(u8)
        mask_row = sb("mask_row", [1, B, S], bf16)

        xn = sb("xn", [P, T, D])
        xl = xn
        cn = sb("cn", [P, T, DC])
        lnT = sb("lnT", [P, T * P])
        xT1 = sb("xT1", [P, T * P])
        cnT = xT1[0:DC, :]
        sq = [part(g, 2048, HALF, 6, HD) for g in range(2)]
        ss = sb("ss", [P, T, 6])
        rq = sb("rq", [P, T, 6])
        qkn = sq
        v0 = [part(g, 5120, HALF * 2, 2, VA) for g in range(2)]
        qT0 = [part(g, 3584, HALF, P) for g in range(2)]
        kT0 = [part(g, 4096, HALF, 2, P) for g in range(2)]
        nm0 = sb("nm0", [P, T * 2], bf16)
        D0 = sb("D0", [P, T * 2, HD], bf16)
        PT0 = [part(g, 0, HALF, 2, 2, P) for g in range(2)]
        rs0 = sb("rs0", [P, T, 2])
        o0 = [part(g, 6160, HALF, D) for g in range(2)]
        oT0 = [part(g, 6672, HALF * P) for g in range(2)]
        xb = sb("xb", [P, T, D])
        x1 = sb("x1", [P, T, D])

        am = sb("am", [P, T])
        scale_x = sb("scale_x", [P, T])
        inv_x = sb("inv_x", [P, T])
        xq = o0
        xqT = lnT
        qT1 = sb("qT1", [P, C1, T * P])
        y, z = qT1[:, 0:C0, :], qT1[:, C0:C1, :]
        w_tmp = qT1[:, 0, :]
        amh = xb[:, :, :].rearrange("p t d -> p (t d)")
        am2 = sb("am2", [P, T])
        scale_z = sb("scale_z", [P, T])
        inv_z = sb("inv_z", [P, T])
        out_z = sb("out_z", [P, T])
        wg = sb("wg", [P, 2])
        zs = y
        zq = [z[:, :, g * 512:g * 512 + 256] for g in range(2)]
        x2 = x

        kT1 = sb("kT1", [P, C1, T * P])
        v1a = sb("v1a", [P, HALF * H1 * VA])
        v1 = (v1a[:, :].rearrange("p (t h d) -> p t h d", t=HALF, h=H1), part(0, 0, HALF, H1, VA))
        nm1 = sb("nm1", [P, 2 * T, C1], bf16)
        ctx_flat = ctx[:, :, :].rearrange("p t d -> p (t d)")
        D1 = ctx_flat[:, 0:512].bitcast(bf16).rearrange("p (i c q) -> p i c q", i=2, c=C1)
        PT1 = part(1, 0, 3, C1, P)
        rs1 = sb("rs1", [P, 2 * T, C1])
        o1 = part(0, 4160, 2 * C1, 2, HD)
        oT1 = part(1, 3072, 2, C1, P)
        x3 = x1

        xT3 = xT1
        ez = sb("ez", [P, T, E])
        sc = sb("sc", [P, T, E])
        biased = sb("biased", [P, T, E])
        gt = ctx_flat[:, 512:576].rearrange("p (e f) -> p e f", f=E)
        eq = ctx_flat[:, 576:640].rearrange("p (e f) -> p e f", f=E)
        rank = sb("rank", [P, T, E])
        cw = sb("cw", [P, T, E])
        cw_half = ctx_flat[:, 640:704].rearrange("p (t e) -> p t e", e=E)
        cw3_half = ctx_flat[:, 704:768].rearrange("p (t e) -> p t e", e=E)
        sl = part(1, 5120, 3, 512)
        h = v1a[:, 0:1536].rearrange("p (i n) -> p i n", i=3)
        hT = v1a[:, 1536:3584].rearrange("p (i e n) -> p i e n", i=4, e=4)
        outb = (part(0, 6208, HALF, D), part(1, 6672, HALF, D))

        bank = [stack.enter_context(nc.psum_tensor(f"bank{i}", [P, 512], f32)) for i in range(BANKS)]
        filled = [sem(f"filled{i}") for i in range(BANKS)]
        taken_sem = [sem(f"taken{i}") for i in range(BANKS)]

        def ps(key):
            return bank[SLOT[key][0]]

        waited = {}

        def wait(eng, semaphore, value):
            if waited.get((eng.engine, semaphore.name), 0) < value:
                waited[eng.engine, semaphore.name] = value
                eng.wait_ge(semaphore, value)

        def full(eng, key):
            wait(eng, filled[SLOT[key][0]], SLOT[key][1])

        def take(ins, key):
            ins.then_inc(taken_sem[SLOT[key][0]], 1)

        def taken(eng, key):
            wait(eng, taken_sem[SLOT[key][0]], SLOT[key][1])

        def batch(b):
            return slice(b * HD, (b + 1) * HD)

        def half_range(g):
            return range(g * HALF, (g + 1) * HALF)

        def half_tiles(g):
            return slice(g * HALF, (g + 1) * HALF)

        def half_tokens(g):
            return slice(g * HALF * P, (g + 1) * HALF * P)

        def counts(name):
            return {step[1:]: n + 1 for n, step in enumerate(x for x in ORDER if x[0] == name)}

        STATS_AT, RSTD_AT, XB_AT = counts("stats"), counts("rstd"), counts("xb")

        for name in """in_wk1 in_wv1 tanh_done wg_done in_x in_ctx in_ctxT in_mask in_w0 in_wq1 in_wo1 in_w1 in_w3
                in_w2 in_gate in_cols in_cols96 in_rows out_done consts dve_step pool_step
                stats_done rstd_done xl_done cn_done gates_done mask_done gq_done wabs_done
                w_up_done w_down_done conv_done sq_done v0_done ss_done rq_done
                D0_done xb_done xq_done y_done amh_done s2_done zq_done xn1_done D1_done
                xn3_done cw_done sl_done""".split():
            sem(name)
        s = sems
        block = stack.enter_context(nc.Block())

        @block.sync
        def _(sp):
            sp.dma_start(x[:, :, :], x_d.rearrange("(t p) d -> p t d", p=P)).then_inc(s["in_x"], 16)
            sp.dma_start(ctxT[:, :], ctxT_d).then_inc(s["in_ctxT"], 16)
            sp.dma_start(wc[:, 0:1280], wc_d[:, 0:1280]).then_inc(s["in_wk1"], 16)
            sp.dma_start(w0[:, :], w0_d).then_inc(s["in_w0"], 16)
            sp.dma_start(wc[:, 1280:2304], wc_d[:, 1280:2304]).then_inc(s["in_wv1"], 16)
            sp.dma_start(w_q1[:, :], wq1_d).then_inc(s["in_wq1"], 16)
            sp.dma_start(w_o1[:, :, :], wo1_d.rearrange("(c p) d -> p c d", p=P)).then_inc(s["in_wo1"], 16)
            sp.dma_start(w_gate[:, :], gate_d).then_inc(s["in_gate"], 16)
            full(sp, ("kT1", 1, C1 - 1))
            full(sp, ("v1", T - 1, 1))
            sp.dma_start(w1, w1_d).then_inc(s["in_w1"], 16)
            sp.dma_start(w3, w3_d).then_inc(s["in_w3"], 16)
            full(sp, ("y0", 1))
            sp.wait_ge(s["w_down_done"], 1)
            sp.dma_start(w2, w2_d.rearrange("p (e d) -> p e d", d=D)).then_inc(s["in_w2"], 16)
            out_v = out_d.rearrange("(t p) d -> p t d", p=P)
            for t in range(T):
                taken(sp, ("f1", t))
                sp.dma_start(out_v[:, t, :], outb[t // HALF][:, t % HALF, :]).then_inc(s["out_done"], 16)
            sp.wait_ge(s["out_done"], 16 * T)

        @block.gpsimd
        def _(pool):
            steps = [0]

            def link(ins):
                steps[0] += 1
                ins.then_inc(s["pool_step"], 1)
                pool.wait_ge(s["pool_step"], steps[0])

            announced = dict(consts=0, rstd_done=0, rq_done=0, D0_done=0, xb_done=0, D1_done=0)

            def announce(ins, name):
                announced[name] += 1
                ins.then_inc(s[name], 1)
                pool.wait_ge(s[name], announced[name])

            link(pool.memset(minus_half[:, :, :], -0.5))
            link(pool.memset(ident[:, :], 0.0))
            link(pool.affine_select(out=ident[:, :], in_=ident[:, :], compare_op=ALU.not_equal, fill=1.0,
                                    base=0, pattern=[[-1, P]], channel_multiplier=1))
            announce(pool.memset(onesf[:, :], 1.0), "consts")

            for step in ORDER:
                name, a = step[0], step[1:]
                if name == "rstd":
                    k, g = a
                    tt = half_tiles(g)
                    var = mv[:, k, tt, 1]
                    wait(pool, s["stats_done"], STATS_AT[k, g])
                    if k == 0:
                        link(pool.tensor_scalar(ln_s[:, 1, tt], var, 1.0 + LN_EPS, LN_EPS * LN_EPS, ALU.mult,
                                                ALU.add))
                        link(pool.tensor_scalar(c_s[:, tt], cmv[:, tt, 1], LN_EPS, None, ALU.add))
                        r, n = ln_s[:, 0:2, tt], 2
                    else:
                        link(pool.tensor_scalar(ln_s[:, k + 1, tt], var, LN_EPS, None, ALU.add))
                        r, n = ln_s[:, k + 1:k + 2, tt], 1
                    announce(pool.tensor_tensor(r, r, minus_half[:, 0:n, :], ALU.pow), "rstd_done")
                elif name == "constants":
                    link(pool.memset(ident64[:, :], 0.0))
                    for b in range(2):
                        link(pool.affine_select(out=ident64[:, :], in_=ident64[:, :], compare_op=ALU.not_equal,
                                                fill=1.0, base=-b * HD, pattern=[[-1, HD]],
                                                channel_multiplier=1))
                    link(pool.memset(blockones[:, :], 0.0))
                    for b in range(2):
                        link(pool.memset(blockones[batch(b), batch(b)], 1.0))
                    link(pool.memset(ones_row[:, :], 1.0))
                    link(pool.memset(before[:, :, :], 1.0))
                    link(pool.affine_select(out=before[:, :, :], in_=before[:, :, :], compare_op=ALU.is_gt,
                                            fill=0.0, base=0, pattern=[[1, E], [-1, E]], channel_multiplier=0))
                    for g in range(2):
                        for b in range(2):
                            link(pool.memset(PT0[g][batch(b), :, :, :, batch(1 - b)], 0.0))
                        link(pool.memset(v0[g][:, :, :, HD:VA], 1.0))
                    announce(pool.memset(v1[0][:, :, :, HD:VA], 1.0), "consts")
                elif name == "biases":
                    pool.wait_ge(s["gates_done"], 1)
                    pool.wait_ge(s["in_rows"], 16)
                    for k, bo in ((0, bo0), (1, bo1)):
                        link(pool.tensor_scalar(bo, bo, gates[:, k:k + 1], None, ALU.mult))
                elif name == "ones_v1":
                    taken(pool, ("oT0", 0))
                    announce(pool.memset(v1[1][:, :, :, HD:VA], 1.0), "consts")
                elif name == "zeros_PT1":
                    taken(pool, ("oT0", 1))
                    for b in range(2):
                        link(pool.memset(PT1[batch(b), :, :, batch(1 - b)], 0.0))
                elif name == "ckv0":
                    t = a[0]
                    pool.wait_ge(s["ss_done"], t + 1)
                    link(pool.tensor_scalar(rq[:, t, :], ss[:, t, :], 1.0 / HD, 1e-16, ALU.mult, ALU.max))
                    announce(pool.tensor_tensor(rq[:, t, :], rq[:, t, :], minus_half_row[:, 0:6], ALU.pow), "rq_done")
                elif name == "D0":
                    r = a[0]
                    taken(pool, ("sm0", r, 0))
                    taken(pool, ("sm0", r, 1))
                    announce(pool.tensor_tensor(
                        D0[:, 4 * r:4 * r + 4, :], ident64[:, :].unsqueeze(1).broadcast_to([P, 4, HD]),
                        nm0[:, 4 * r:4 * r + 4].unsqueeze(2).broadcast_to([P, 4, HD]), ALU.mult), "D0_done")
                elif name == "xb":
                    k, g = a
                    if k == 1:
                        pool.wait_ge(s["stats_done"], STATS_AT[2, g])
                    announce(pool.tensor_tensor(xb[:, half_tiles(g), :], (x, x2)[k][:, half_tiles(g), :],
                                                (bo0, bo1)[k].unsqueeze(1).broadcast_to([P, HALF, D]), ALU.add),
                             "xb_done")
                elif name == "sm1":
                    i = a[0]
                    taken(pool, ("sm1", i))
                    if i >= 2:
                        full(pool, ("sT1", i - 2))
                    announce(pool.tensor_tensor(
                        D1[:, i % 2, :, :], ident64[:, :].unsqueeze(1).broadcast_to([P, C1, HD]),
                        nm1[:, i, :].unsqueeze(2).broadcast_to([P, C1, HD]), ALU.mult), "D1_done")

        @block.scalar
        def _(act):
            act.dma_start(ctx[:, :, :], ctx_d.rearrange("(t p) d -> p t d", p=P)).then_inc(s["in_ctx"], 16)
            act.dma_start(rows[:, :], rows_d.broadcast_to([P, 268])).then_inc(s["in_rows"], 16)
            act.dma_start(cols[:, :], cols_d).then_inc(s["in_cols"], 16)
            act.dma_start(cols96[:, :], cols96_d).then_inc(s["in_cols96"], 16)
            act.dma_start(mask8[:, :], mask_d).then_inc(s["in_mask"], 16)

            wait(act, s["in_rows"], 16)
            act.activation(gates[:, :], gates_raw, ACT.Tanh).then_inc(s["gates_done"], 1)
            wait(act, s["in_cols96"], 16)
            wait(act, s["in_cols"], 16)

            def heads(ap):
                return ap.rearrange("p (h d) -> p h d", d=HD)

            for step in ORDER:
                name, a = step[0], step[1:]
                if name in ("cnT", "lnT", "kT1", "v1", "qkv0", "ckv0", "qkT0", "sT0", "oT0", "xqT", "h0", "xT1",
                            "sT1", "oT1", "xT3", "gate", "G", "hT") or (name == "qT1" and a[1] % 2 == 0):
                    full(act, step)
                    out = ps(step)
                if name == "cnT":
                    take(act.activation(cnT[:, half_tokens(a[0])], out[0:DC, :], ACT.Identity,
                                        scale=cols96[:, 0:1], bias=cols96[:, 1:2]), step)
                elif name == "lnT":
                    take(act.activation(lnT[:, half_tokens(a[0])], out[:, :], ACT.Identity, scale=lnl_g,
                                        bias=lnl_b), step)
                elif name == "kT1":
                    g, c = a
                    take(act.activation(kT1[:, c, half_tokens(g)], out[:, :], ACT.Copy), step)
                elif name == "v1":
                    t, j = a
                    wait(act, s["consts"], 2 + t // HALF)
                    take(act.activation(v1[t // HALF][:, t % HALF, 8 * j:8 * j + 8, 0:HD], heads(out[:, :]),
                                        ACT.Copy), step)
                elif name == "qkv0":
                    g, n = divmod(a[0], HALF)
                    act.activation(sq[g][:, n, 0:4, :], heads(out[:, 0:256]), ACT.Square)\
                       .then_inc(s["sq_done"], 1)
                    wait(act, s["consts"], 2)
                    act.activation(v0[g][:, 2 * n + 1, :, 0:HD], heads(out[:, 256:384]), ACT.Copy)\
                       .then_inc(s["v0_done"], 1)
                elif name == "ckv0":
                    g, n = divmod(a[0], HALF)
                    act.activation(sq[g][:, n, 4:6, :], heads(out[:, 0:128]), ACT.Square)\
                       .then_inc(s["sq_done"], 1)
                    act.activation(v0[g][:, 2 * n, :, 0:HD], heads(out[:, 128:256]), ACT.Copy)\
                       .then_inc(s["v0_done"], 1)
                elif name == "qkT0":
                    g, n = divmod(a[0], HALF)
                    act.activation(kT0[g][:, n, :, :], out[:, 128:384].rearrange("p (g n) -> p g n", g=2), ACT.Copy)
                    wait(act, s["gq_done"], 1)
                    take(act.activation(qT0[g][:, n, :], out[:, 0:128], ACT.Copy, scale=gq[:, 0:1]), step)
                elif name == "sT0":
                    r, hh = a
                    g, n = divmod(2 * r, HALF)
                    for b in range(2):
                        i = act.activation(PT0[g][batch(b), n:n + 2, :, hh, batch(b)],
                                           out[batch(b), 0:256].rearrange("p (t g q) -> p t g q", t=2, g=2),
                                           ACT.Exp)
                    take(i, step)
                elif name == "oT0":
                    take(act.activation(oT0[a[0]], out[:, :], ACT.Copy), step)
                elif name == "xqT":
                    take(act.activation(xqT[:, half_tokens(a[0])], out[:, :], ACT.Copy), step)
                elif name == "h0":
                    g, c = a
                    wait(act, s["conv_done"], 1)
                    act.activation(y[:, c, half_tokens(g)], out[:, :], ACT.Identity, scale=conv_ws[:, c, 1:2],
                                   bias=conv_b[:, c:c + 1]).then_inc(s["y_done"], 1)
                elif name == "silu0":
                    g, c = a
                    taken(act, ("h0", g, c))
                    act.activation(z[:, c, half_tokens(g)], y[:, c, half_tokens(g)], ACT.Tanh, scale=0.5)\
                       .then_inc(s["tanh_done"], 1)
                elif name in ("xT1", "xT3"):
                    take(act.activation(xT1[:, half_tokens(a[0])], out[:, :], ACT.Copy), step)
                elif name == "qT1" and a[1] % 2 == 0:
                    g, c = a
                    take(act.activation(qT1[:, c, half_tokens(g)], out[:, :], ACT.Copy, scale=HD**-0.5), step)
                elif name == "sT1":
                    unit = a[0]
                    if unit >= 3:
                        full(act, ("pv1", unit - 3, 1))
                    for b in range(2):
                        i = act.activation(PT1[batch(b), unit % 3, :, batch(b)], heads(out[batch(b), :]), ACT.Exp)
                    take(i, step)
                elif name == "oT1":
                    t, j = a
                    if t >= 2:
                        full(act, ("y1", t - 2))
                    take(act.activation(oT1[:, t % 2, 4 * j:4 * j + 4, :],
                                        out[:, :].rearrange("p (c n) -> p c n", n=P), ACT.Copy), step)
                elif name == "gate":
                    take(act.activation(ez[:, half_tiles(a[0]), :],
                                        out[:, 0:32].rearrange("p (t e) -> p t e", e=E), ACT.Exp, scale=-1.0), step)
                elif name == "G":
                    t, j = divmod(a[0], 3)
                    wait(act, s["cw_done"], t // HALF + 1)
                    if a[0] >= 3:
                        taken(act, ("U", a[0] - 3))
                    for e in range(4 if j < 2 else 1):
                        scale = cw_half[:, t, 4 * j + e:4 * j + e + 1] if j < 2 else 0.5
                        i = act.activation(sl[:, a[0] % 3, e * P:(e + 1) * P], out[:, e * P:(e + 1) * P], ACT.Tanh,
                                           scale=scale)
                    i.then_inc(s["sl_done"], 1)
                elif name == "hT":
                    unit = a[0]
                    if unit >= 4:
                        full(act, ("f1", (unit - 4) // 3))
                    n = 1 if unit % 3 == 2 else 4
                    take(act.activation(hT[:, unit % 4, 0:n, :], out[:, 0:n * P].rearrange("p (e n) -> p e n", n=P),
                                        ACT.Copy), step)

        @block.vector
        def _(dve):
            steps = [0]

            def link(ins):
                steps[0] += 1
                ins.then_inc(s["dve_step"], 1)
                dve.wait_ge(s["dve_step"], steps[0])

            def heads(ap, d=HD):
                return ap.rearrange("p (h d) -> p h d", d=d)

            def apply_ln(k, t, src, dst):
                return dve.tensor_scalar(dst[:, t, :], src[:, t, :], mv[:, k, t, 0:1], ln_s[:, k + 1, t:t + 1],
                                         ALU.subtract, ALU.mult)

            def wait_rstd(k, g):
                dve.wait_ge(s["rstd_done"], RSTD_AT[k, g])

            for step in ORDER:
                name, a = step[0], step[1:]
                if name in ("wsum", "sm0", "pv0", "y0", "h0", "amT", "s2b", "f0", "sm1", "pv1", "y1", "U",
                            "f1") or (name == "qT1" and a[1] % 2 == 1):
                    full(dve, step)
                    out = ps(step)
                if name == "stats":
                    k, g = a
                    src = (x, x1, x2, x3)[k]
                    if k == 0:
                        dve.wait_ge(s["in_ctx"], 16)
                        for t in half_range(g):
                            i = dve.bn_stats(cstats[:, t, :], ctx[:, t, :])
                        link(i)
                        for t in half_range(g):
                            i = dve.bn_aggr(cmv[:, t, :], cstats[:, t, :])
                        dve.wait_ge(s["in_x"], 16)
                    else:
                        taken(dve, {1: ("y0", g), 2: ("f0", g), 3: ("y1", half_range(g)[-1])}[k])
                    for t in half_range(g):
                        i = dve.bn_stats(stats[:, t, :], src[:, t, :])
                    link(i)
                    for t in half_range(g):
                        i = dve.bn_aggr(mv[:, k, t, :], stats[:, t, :])
                    i.then_inc(s["stats_done"], 1)
                elif name == "norm0":
                    g = a[0]
                    wait_rstd(0, g)
                    for t in half_range(g):
                        i = dve.tensor_scalar(cn[:, t, :], ctx[:, t, :], cmv[:, t, 0:1], c_s[:, t:t + 1],
                                              ALU.subtract, ALU.mult)
                    i.then_inc(s["cn_done"], 1)
                    for t in half_range(g):
                        i = apply_ln(0, t, x, xn)
                    i.then_inc(s["xl_done"], 1)
                elif name == "wabs":
                    dve.wait_ge(s["in_mask"], 16)
                    dve.tensor_scalar(mask_row[:, :, :], mask8[:, :].rearrange("p (b k) -> p b k", k=S), 1.0, -BIG,
                                      ALU.subtract, ALU.mult).then_inc(s["mask_done"], 1)
                    dve.wait_ge(s["in_cols"], 16)
                    dve.scalar_tensor_tensor(gq[:, :], qn_g, HD**-0.5, kn_g, ALU.mult, ALU.mult)\
                       .then_inc(s["gq_done"], 1)
                    dve.wait_ge(s["in_w0"], 16)
                    dve.tensor_reduce(wabs[:, 0:1], w_up, AX.X, ALU.add, apply_absolute_value=True)
                    dve.tensor_reduce(wabs[:, 1:2], w_down, AX.X, ALU.add, apply_absolute_value=True)\
                       .then_inc(s["wabs_done"], 1)
                elif name == "wsum":
                    take(dve.tensor_scalar(winv[:, :], out[:, 0:2], 1.0 / (D * HID0), 1e-5, ALU.mult, ALU.max),
                         step)
                    taken(dve, step)
                    link(dve.reciprocal(wsc[:, :], winv[:, :]))
                    for k, wsrc in enumerate((w_up, w_down)):
                        tmp = w_tmp[:, 512 * k:512 * k + 512]
                        link(dve.tensor_scalar(tmp, wsrc, wsc[:, k:k + 1], MAGIC, ALU.mult, ALU.add))
                        link(dve.tensor_scalar(tmp, tmp, MAGIC, 1.0, ALU.subtract, ALU.min))
                    dve.tensor_scalar(w_upq[:, :], w_tmp[:, 0:512], -1.0, None, ALU.max)\
                       .then_inc(s["w_up_done"], 1)
                    dve.tensor_scalar(w_downq[:, :, :], w_tmp[:, 512:1024].rearrange("p (c d) -> p c d", d=D), -1.0,
                                      None, ALU.max).then_inc(s["w_down_done"], 1)
                    dve.tensor_scalar(conv_ws[:, :, :], conv_w, winv[:, 0:1], None, ALU.mult)\
                       .then_inc(s["conv_done"], 1)
                elif name == "ckv0":
                    g, n = divmod(a[0], HALF)
                    dve.wait_ge(s["sq_done"], 2 * a[0] + 2)
                    dve.tensor_reduce(ss[:, a[0], :], sq[g][:, n, :, :], AX.X, ALU.add).then_inc(s["ss_done"], 1)
                elif name == "norm_qk":
                    t = a[0]
                    g, n = divmod(t, HALF)
                    kq, kc = ("qkv0", t), ("ckv0", t)
                    dve.wait_ge(s["rq_done"], t + 1)
                    dve.wait_ge(s["v0_done"], 2 * t + 2)
                    take(dve.tensor_tensor(qkn[g][:, n, 0:4, :], heads(ps(kq)[:, 0:256]),
                                           rq[:, t, 0:4].unsqueeze(2).broadcast_to([P, 4, HD]), ALU.mult), kq)
                    take(dve.tensor_tensor(qkn[g][:, n, 4:6, :], heads(ps(kc)[:, 0:128]),
                                           rq[:, t, 4:6].unsqueeze(2).broadcast_to([P, 2, HD]), ALU.mult), kc)
                elif name == "sm0":
                    r, hh = a
                    take(dve.tensor_reduce(nm0[:, 4 * r + hh:4 * r + hh + 3:2],
                                           out[:, 0:256].rearrange("p (t k) -> p t k", t=2), AX.X, ALU.max,
                                           negate=True), step)
                elif name == "pv0":
                    t = a[0]
                    g, n = divmod(t, HALF)
                    o_ps = heads(out[:, 0:2 * VA], VA)
                    link(dve.reciprocal(rs0[:, t, :], o_ps[:, :, HD]))
                    take(dve.tensor_tensor(heads(o0[g][:, n, :]), o_ps[:, :, 0:HD],
                                           rs0[:, t, :].unsqueeze(2).broadcast_to([P, 2, HD]), ALU.mult), step)
                elif name == "y0":
                    g = a[0]
                    tt = half_tiles(g)
                    dve.wait_ge(s["xb_done"], XB_AT[0, g])
                    take(dve.scalar_tensor_tensor(x1[:, tt, :], heads(out[:, :], D), gates[:, 0:1], xb[:, tt, :],
                                                  ALU.mult, ALU.add), step)
                elif name == "quant":
                    g = a[0]
                    tt = half_tiles(g)
                    wait_rstd(1, g)
                    for t in half_range(g):
                        i = apply_ln(1, t, x1, xn)
                    link(i)
                    link(dve.tensor_reduce(am[:, tt], xn[:, tt, :], AX.X, ALU.max, apply_absolute_value=True))
                    link(dve.tensor_scalar(inv_x[:, tt], am[:, tt], 1e-5, 1.0 / 127.0, ALU.max, ALU.mult))
                    link(dve.reciprocal(scale_x[:, tt], inv_x[:, tt]))
                    for t in half_range(g):
                        i = dve.tensor_scalar(xn[:, t, :], xn[:, t, :], scale_x[:, t:t + 1], MAGIC, ALU.mult, ALU.add)
                    link(i)
                    for t in half_range(g):
                        i = dve.tensor_scalar(xq[g][:, t % HALF, :], xn[:, t, :], MAGIC, inv_x[:, t:t + 1],
                                              ALU.subtract, ALU.mult)
                    i.then_inc(s["xq_done"], 1)
                elif name == "h0":
                    g, c = a
                    hv = heads(out[:, :], S)
                    yv = heads(y[:, c, half_tokens(g)], S)
                    dve.wait_ge(s["y_done"], g * C0 + c + 1)
                    link(dve.scalar_tensor_tensor(yv[:, :, 1:S], hv[:, :, 0:S - 1], conv_ws[:, c, 0:1],
                                                  yv[:, :, 1:S], ALU.mult, ALU.add))
                    take(dve.scalar_tensor_tensor(yv[:, :, 0:S - 1], hv[:, :, 1:S], conv_ws[:, c, 2:3],
                                                  yv[:, :, 0:S - 1], ALU.mult, ALU.add), step)
                elif name == "silu0":
                    g, c = a
                    dve.wait_ge(s["tanh_done"], g * C0 + c + 1)
                    i = dve.scalar_tensor_tensor(z[:, c, half_tokens(g)], z[:, c, half_tokens(g)], 1.0,
                                                 y[:, c, half_tokens(g)], ALU.add, ALU.mult)
                    if c == C0 - 1:
                        link(i)
                elif name == "amh":
                    dve.tensor_reduce(amh[:, half_tokens(a[0])],
                                      z[:, :, half_tokens(a[0])].rearrange("p c n -> p n c"), AX.X, ALU.max,
                                      apply_absolute_value=True).then_inc(s["amh_done"], 1)
                elif name == "amT":
                    g = a[0]
                    tt = half_tiles(g)
                    take(dve.tensor_reduce(am2[:, tt], heads(out[:, :], P), AX.X, ALU.max), step)
                    taken(dve, step)
                    link(dve.tensor_scalar(inv_z[:, tt], am2[:, tt], 2e-5, 1.0 / 127.0, ALU.max, ALU.mult))
                    dve.reciprocal(scale_z[:, tt], inv_z[:, tt]).then_inc(s["s2_done"], 1)
                    dve.tensor_scalar(wg[:, g:g + 1], winv[:, 1:2], gates[:, 2:3], 0.5, ALU.mult, ALU.mult)\
                       .then_inc(s["wg_done"], 1)
                    dve.wait_ge(s["wg_done"], g + 1)
                    link(dve.tensor_scalar(out_z[:, tt], inv_z[:, tt], wg[:, g:g + 1], None, ALU.mult))
                elif name == "s2b":
                    g = a[0]
                    for c in range(C0):
                        i = dve.tensor_tensor(zs[:, c, half_tokens(g)], z[:, c, half_tokens(g)], out[:, :],
                                              ALU.mult)
                    take(i, step)
                    taken(dve, step)
                    dve.tensor_scalar(zq[g].bitcast(bf16), zs[:, :, half_tokens(g)], MAGIC, MAGIC, ALU.add,
                                      ALU.subtract).then_inc(s["zq_done"], 1)
                elif name == "f0":
                    g = a[0]
                    for t in half_range(g):
                        i = dve.scalar_tensor_tensor(x2[:, t, :], out[:, (t % HALF) * D:(t % HALF + 1) * D],
                                                     out_z[:, t:t + 1], x1[:, t, :], ALU.mult, ALU.add)
                    take(i, step)
                elif name in ("norm1", "norm3"):
                    k = 2 if name == "norm1" else 3
                    wait_rstd(k, a[0])
                    for t in half_range(a[0]):
                        i = apply_ln(k, t, (x2, x3)[k - 2], xn)
                    i.then_inc(s["xn1_done" if k == 2 else "xn3_done"], 1)
                elif name == "qT1" and a[1] % 2 == 1:
                    g, c = a
                    take(dve.tensor_scalar(qT1[:, c, half_tokens(g)], out[:, :], HD**-0.5, None, ALU.mult), step)
                elif name == "sm1":
                    take(dve.tensor_reduce(nm1[:, a[0], :], heads(out[:, :]), AX.X, ALU.max, negate=True), step)
                elif name == "pv1":
                    unit, q = a
                    t, par = divmod(unit, 2)
                    if par == 0 and q == 0 and t >= 2:
                        full(dve, ("oT1", t - 2, 1))
                    o_ps = heads(out[:, 0:4 * VA], VA)
                    r = rs1[:, unit, 4 * q:4 * q + 4]
                    row = C1 * (t % 2) + 4 * q
                    link(dve.reciprocal(r, o_ps[:, :, HD]))
                    take(dve.tensor_tensor(o1[:, row:row + 4, par, :], o_ps[:, :, 0:HD],
                                           r.unsqueeze(2).broadcast_to([P, 4, HD]), ALU.mult), step)
                elif name == "y1":
                    t = a[0]
                    dve.wait_ge(s["xb_done"], XB_AT[1, t // HALF])
                    take(dve.scalar_tensor_tensor(x3[:, t, :], out[:, 0:D], gates[:, 1:2], xb[:, t, :], ALU.mult,
                                                  ALU.add), step)
                elif name == "router":
                    g = a[0]
                    tt = half_tiles(g)
                    taken(dve, ("gate", g))
                    link(dve.tensor_scalar(ez[:, tt, :], ez[:, tt, :], 1.0, None, ALU.add))
                    link(dve.reciprocal(sc[:, tt, :], ez[:, tt, :]))
                    link(dve.tensor_tensor(biased[:, tt, :], sc[:, tt, :],
                                           e_bias.unsqueeze(1).broadcast_to([P, HALF, E]), ALU.add))
                    for t in half_range(g):
                        this = biased[:, t, :].unsqueeze(2).broadcast_to([P, E, E])
                        other = biased[:, t, :].unsqueeze(1).broadcast_to([P, E, E])
                        dve.tensor_tensor(gt[:, :, :], other, this, ALU.is_gt)
                        link(dve.tensor_tensor(eq[:, :, :], other, this, ALU.is_equal))
                        link(dve.tensor_tensor(eq[:, :, :], eq[:, :, :], before[:, :, :], ALU.mult))
                        link(dve.tensor_tensor(gt[:, :, :], gt[:, :, :], eq[:, :, :], ALU.add))
                        link(dve.tensor_reduce(rank[:, t, :], gt[:, :, :], AX.X, ALU.add))
                    link(dve.scalar_tensor_tensor(cw[:, tt, :], rank[:, tt, :], 2.0, sc[:, tt, :], ALU.is_lt,
                                                  ALU.mult))
                    link(dve.tensor_scalar(cw_half[:, tt, :], cw[:, tt, :], 0.5, None, ALU.mult))
                    link(dve.tensor_tensor(cw3_half[:, tt, :], cw[:, tt, :], cw_half[:, tt, :], ALU.mult))
                    dve.tensor_tensor(cw3_half[:, tt, :], cw3_half[:, tt, :], cw[:, tt, :], ALU.mult)\
                       .then_inc(s["cw_done"], 1)
                elif name == "U":
                    unit = a[0]
                    t, j = divmod(unit, 3)
                    dve.wait_ge(s["sl_done"], unit + 1)
                    if unit >= 3:
                        full(dve, ("hT", unit - 3))
                    n = 512 if j < 2 else 128
                    buf = unit % 3
                    take(dve.scalar_tensor_tensor(sl[:, buf, 0:n], sl[:, buf, 0:n], 1.0, ps(("G", unit))[:, 0:n],
                                                  ALU.add, ALU.mult), ("G", unit))
                    taken(dve, ("G", unit))
                    for e in range(n // P):
                        k = slice(e * P, (e + 1) * P)
                        scale = cw3_half[:, t, 4 * j + e:4 * j + e + 1] if j < 2 else 0.5
                        i = dve.scalar_tensor_tensor(h[:, buf, k], out[:, k], scale, sl[:, buf, k], ALU.mult,
                                                     ALU.mult)
                    take(i, step)
                elif name == "f1":
                    t = a[0]
                    take(dve.scalar_tensor_tensor(outb[t // HALF][:, t % HALF, :], out[:, 0:D], gates[:, 3:4],
                                                  x3[:, t, :], ALU.mult, ALU.add), step)

        @block.tensor
        def _(pe):
            def transposes(key, sources, n_out=P):
                for n, src in enumerate(sources):
                    i = pe.transpose(ps(key)[0:n_out, n * P:(n + 1) * P], src, ident[:, :])
                return i

            def mm(out, lhsT, rhs, start=True, stop=True):
                return pe.matmul(out, lhsT, rhs, start=start, stop=stop, skip_group_check=True)

            def tok(t, b=None):
                return slice(t * P, (t + 1) * P) if b is None else slice(t * P + b * S, t * P + (b + 1) * S)

            wait(pe, s["consts"], 1)
            for n, key in enumerate(RESULTS):
                name, a = key[0], key[1:]
                out = ps(key)
                if n >= BANKS:
                    taken(pe, RESULTS[n - BANKS])
                if name == "cnT":
                    wait(pe, s["cn_done"], a[0] + 1)
                    i = transposes(key, [cn[:, t, :] for t in half_range(a[0])], DC)
                elif name == "lnT":
                    wait(pe, s["xl_done"], a[0] + 1)
                    i = transposes(key, [xn[:, t, :] for t in half_range(a[0])])
                elif name == "wsum":
                    wait(pe, s["wabs_done"], 1)
                    i = mm(out[:, 0:2], onesf[:, :], wabs[:, :])
                elif name == "kT1":
                    g, c = a
                    wait(pe, s["in_wk1"], 16)
                    wait(pe, s["in_ctxT"], 16)
                    i = mm(out[:, :], w_k1[:, c * P:(c + 1) * P], ctxT[:, half_tokens(g)])
                elif name == "v1":
                    t, j = a
                    wait(pe, s["in_wv1"], 16)
                    i = mm(out[:, :], ctxT[:, tok(t)], w_v1[:, 512 * j:512 * (j + 1)])
                elif name == "qkv0":
                    t = a[0]
                    wait(pe, s["in_w0"], 16)
                    taken(pe, ("lnT", t // HALF))
                    i = mm(out[:, 0:384], lnT[:, tok(t)], w_qlkv)
                elif name == "ckv0":
                    t = a[0]
                    wait(pe, s["in_wk1"], 16)
                    taken(pe, ("cnT", t // HALF))
                    i = mm(out[:, 0:256], cnT[:, tok(t)], w_ckv)
                elif name == "qkT0":
                    g, n_ = divmod(a[0], HALF)
                    taken(pe, ("ckv0", a[0]))
                    taken(pe, ("qkv0", a[0]))
                    i = transposes(key, [qkn[g][:, n_, 2 * c:2 * c + 2, :].rearrange("p h d -> p (h d)")
                                         for c in (0, 2, 1)])
                elif name == "sm0":
                    r, hh = a
                    hr = batch(hh)
                    g, n_ = divmod(2 * r, HALF)
                    wait(pe, s["mask_done"], 1)
                    wait(pe, s["consts"], 2)
                    taken(pe, ("qkT0", 2 * r))
                    taken(pe, ("qkT0", 2 * r + 1))
                    for b in range(2):
                        for m in range(2):
                            mm(out[batch(b), m * P:m * P + S], ones_row[0:1, 0:HD],
                               mask_row[0:1, 4 * r + 2 * m + b, :], start=m == 0, stop=False)
                    for m in range(2):
                        for grp in range(2):
                            for b in range(2):
                                c = m * P + grp * S
                                i = mm(out[batch(b), c:c + S], qT0[g][hr, n_ + m, batch(b)],
                                       kT0[g][hr, n_ + m, grp, batch(b)], start=False)
                elif name == "sT0":
                    r, hh = a
                    hr = batch(hh)
                    g, n_ = divmod(2 * r, HALF)
                    wait(pe, s["D0_done"], r + 1)
                    mm(out[:, 0:256], blockones[:, :],
                       D0[:, 4 * r + hh:4 * r + hh + 3:2, :].unsqueeze(2).broadcast_to([P, 2, 2, HD]), stop=False)
                    for m in range(2):
                        t = 2 * r + m
                        mm(out[:, m * P:m * P + S],
                           mask_row[0:1, 2 * t:2 * t + 2, :].rearrange("p b k -> p (b k)"), ones_row[0:1, 0:HD],
                           start=False, stop=False)
                    for m in range(2):
                        for grp in range(2):
                            for b in range(2):
                                c = m * P + grp * S
                                i = mm(out[batch(b), c:c + S], kT0[g][hr, n_ + m, grp, batch(b)],
                                       qT0[g][hr, n_ + m, batch(b)], start=False)
                elif name == "pv0":
                    g, n_ = divmod(a[0], HALF)
                    taken(pe, ("sT0", a[0] // 2, 0))
                    taken(pe, ("sT0", a[0] // 2, 1))
                    for hh in range(2):
                        for grp in range(2):
                            i = mm(out[:, hh * VA:(hh + 1) * VA], PT0[g][:, n_, grp, hh, :],
                                   v0[g][:, 2 * n_ + grp, hh, :], start=grp == 0, stop=grp == 1)
                elif name == "oT0":
                    for t in half_range(a[0]):
                        taken(pe, ("pv0", t))
                    i = transposes(key, [o0[a[0]][:, m, :] for m in range(HALF)])
                elif name == "y0":
                    taken(pe, ("oT0", a[0]))
                    for m in range(HALF):
                        i = mm(out[:, m * D:(m + 1) * D], oT0[a[0]][:, m * P:(m + 1) * P], w_o0)
                elif name == "xqT":
                    wait(pe, s["xq_done"], a[0] + 1)
                    i = transposes(key, [xq[a[0]][:, m, :] for m in range(HALF)])
                elif name == "h0":
                    g, c = a
                    wait(pe, s["w_up_done"], 1)
                    taken(pe, ("xqT", g))
                    i = mm(out[:, :], w_upq[:, c * P:(c + 1) * P], xqT[:, half_tokens(g)])
                elif name == "amT":
                    wait(pe, s["amh_done"], a[0] + 1)
                    i = transposes(key, [amh[:, tok(t)] for t in half_range(a[0])])
                elif name == "s2b":
                    wait(pe, s["s2_done"], a[0] + 1)
                    for m, t in enumerate(half_range(a[0])):
                        i = mm(out[:, m * P:(m + 1) * P], scale_z[:, t:t + 1].broadcast_to([P, P]), ident[:, :])
                elif name == "f0":
                    wait(pe, s["zq_done"], a[0] + 1)
                    wait(pe, s["w_down_done"], 1)
                    zb = zq[a[0]].bitcast(bf16)
                    for m in range(HALF):
                        for c in range(C0):
                            i = mm(out[:, m * D:(m + 1) * D], zb[:, c, m * P:(m + 1) * P], w_downq[:, c, :],
                                   start=c == 0, stop=c == C0 - 1)
                elif name == "xT1":
                    wait(pe, s["xn1_done"], a[0] + 1)
                    i = transposes(key, [xn[:, t, :] for t in half_range(a[0])])
                elif name == "qT1":
                    g, c = a
                    wait(pe, s["in_wq1"], 16)
                    taken(pe, ("xT1", g))
                    i = mm(out[:, :], w_q1[:, c * P:(c + 1) * P], xT1[:, half_tokens(g)])
                elif name == "sm1":
                    t, par = divmod(a[0], 2)
                    hr = batch(par)
                    for c in range(C1):
                        taken(pe, ("qT1", t // HALF, c))
                        taken(pe, ("kT1", t // HALF, c))
                        for b in range(2):
                            i = mm(out[batch(b), c * HD:(c + 1) * HD], qT1[hr, c, tok(t, b)], kT1[hr, c, tok(t, b)])
                elif name == "sT1":
                    t, par = divmod(a[0], 2)
                    hr = batch(par)
                    wait(pe, s["D1_done"], a[0] + 1)
                    mm(out[:, :], blockones[:, :], D1[:, a[0] % 2, :, :].rearrange("p c q -> p (c q)"), stop=False)
                    for c in range(C1):
                        for b in range(2):
                            i = mm(out[batch(b), c * HD:(c + 1) * HD], kT1[hr, c, tok(t, b)], qT1[hr, c, tok(t, b)],
                                   start=False)
                elif name == "pv1":
                    unit, q = a
                    t, par = divmod(unit, 2)
                    taken(pe, ("sT1", unit))
                    taken(pe, ("v1", t, 0))
                    taken(pe, ("v1", t, 1))
                    for m in range(4):
                        c = 4 * q + m
                        i = mm(out[:, m * VA:(m + 1) * VA], PT1[:, unit % 3, c, :],
                               v1[t // HALF][:, t % HALF, 2 * c + par, :])
                elif name == "oT1":
                    t, j = a
                    for par in range(2):
                        for q in range(2):
                            taken(pe, ("pv1", 2 * t + par, q))
                    i = transposes(key, [o1[:, C1 * (t % 2) + c, :, :].rearrange("p r d -> p (r d)")
                                         for c in range(4 * j, 4 * j + 4)])
                elif name == "y1":
                    t = a[0]
                    wait(pe, s["in_wo1"], 16)
                    taken(pe, ("oT1", t, 0))
                    taken(pe, ("oT1", t, 1))
                    for c in range(C1):
                        i = mm(out[:, 0:D], oT1[:, t % 2, c, :], w_o1[:, c, :], start=c == 0, stop=c == C1 - 1)
                elif name == "xT3":
                    wait(pe, s["xn3_done"], a[0] + 1)
                    i = transposes(key, [xn[:, t, :] for t in half_range(a[0])])
                elif name == "gate":
                    wait(pe, s["in_gate"], 16)
                    taken(pe, ("xT3", a[0]))
                    for m, t in enumerate(half_range(a[0])):
                        i = mm(out[:, m * E:(m + 1) * E], xT3[:, tok(t)], w_gate[:, :])
                elif name in ("G", "U"):
                    t, j = divmod(a[0], 3)
                    w, loaded = (w1, "in_w1") if name == "G" else (w3, "in_w3")
                    wait(pe, s[loaded], 16)
                    taken(pe, ("xT3", t // HALF))
                    n_out = 512 if j < 2 else 128
                    i = mm(out[:, 0:n_out], xT3[:, tok(t)], w[:, 512 * j:512 * j + n_out])
                elif name == "hT":
                    taken(pe, ("U", a[0]))
                    i = transposes(key, [h[:, a[0] % 3, e * P:(e + 1) * P] for e in range(1 if a[0] % 3 == 2 else 4)])
                elif name == "f1":
                    t = a[0]
                    wait(pe, s["in_w2"], 16)
                    for e in range(EN):
                        k = 3 * t + e // 4
                        if e % 4 == 0:
                            taken(pe, ("hT", k))
                        i = mm(out[:, 0:D], hT[:, k % 4, e % 4, :], w2[:, e, :], start=e == 0, stop=e == EN - 1)
                i.then_inc(filled[SLOT[key][0]], 1)


def kernel(**inputs):
    import numpy as np
    import concourse.bacc as bacc
    from concourse import mybir
    from concourse.bass_utils import run_bass_kernel_spmd

    v = {k: np.asarray(a) for k, a in inputs.items()}
    tr = lambda a: np.ascontiguousarray(a.T)
    cat = lambda *a: np.ascontiguousarray(np.concatenate(a, axis=1))
    col = lambda a: np.asarray(a).reshape(-1, 1)
    w2_0 = tr(v["L0_ffn_w2"]).reshape(C0, P, D).transpose(1, 0, 2).reshape(P, C0 * D)
    experts = lambda w, sw: cat(*[tr(w[e]) for e in range(E)], tr(sw))
    qn, kn = v["L0_xattn_qn_g"], v["L0_xattn_kn_g"]
    arrays = {
        "x": v["x"].reshape(B * S, D),
        "ctx": v["ctx_768"].reshape(B * S, DC),
        "ctxT": tr(v["ctx_768"].reshape(B * S, DC)),
        "mask": v["mask_BxS2_bk0"].reshape(1, B * S),
        "w0": cat(tr(v["L0_xattn_Wq"]), tr(v["L0_xattn_Wlkv"]), tr(v["L0_xattn_Wo"]), tr(v["L0_ffn_w1"]), w2_0),
        "wc": cat(tr(v["L0_xattn_Wkv"]), v["L1_xattn_Wk"], v["L1_xattn_Wv"]),
        "wq1": np.ascontiguousarray(v["L1_xattn_Wq"]),
        "wo1": np.ascontiguousarray(v["L1_xattn_Wo"]),
        "w1": experts(v["L1_ffn_w1"], v["L1_ffn_sw1"]),
        "w3": experts(v["L1_ffn_w3"], v["L1_ffn_sw3"]),
        "w2": experts(v["L1_ffn_w2"], v["L1_ffn_sw2"]),
        "gate": tr(v["L1_ffn_gate_w"]),
        "cols": cat(col(v["L0_xattn_ln_l_g"]), col(v["L0_xattn_ln_l_b"]), col(np.concatenate([qn, qn])),
                    col(np.concatenate([kn, kn])),
                    v["L0_ffn_conv_w"].reshape(C0, P, 3).transpose(1, 0, 2).reshape(P, C0 * 3),
                    v["L0_ffn_conv_b"].reshape(C0, P).T),
        "cols96": cat(col(v["L0_xattn_ln_x_g"]), col(v["L0_xattn_ln_x_b"])),
        "rows": np.concatenate([v["L0_xattn_bo"], v["L1_xattn_bo"], v["L1_ffn_expert_bias"], v["g_xattn"],
                                v["g_ffn"]]).reshape(1, -1),
    }
    nc = bacc.Bacc("TRN2", target_bir_lowering=False, num_devices=1)
    args = [nc.dram_tensor(f"in_{k}_dram", a.shape, mybir.dt.from_np(a.dtype), kind="ExternalInput").ap()
            for k, a in arrays.items()]
    out = nc.dram_tensor("out_dram", (B * S, D), mybir.dt.float32, kind="ExternalOutput").ap()
    build_program(nc, *args, out)
    r = run_bass_kernel_spmd(nc, [{f"in_{k}_dram": a for k, a in arrays.items()}], core_ids=[0])
    return r.results[0]["out_dram"].reshape(B, S, D)
```
